# Optimizing a Trainium2 kernel written in Bass

```python
import numpy as np
import jax
import jax.numpy as jnp

def _softmax(x, axis=-1):
    return jax.nn.softmax(x, axis=axis)

def _gelu(x):
    return jax.nn.gelu(x, approximate=True)

def _silu(x):
    return jax.nn.silu(x)

def _sigmoid(x):
    return jax.nn.sigmoid(x)

def _layernorm(x, axis=-1, eps=1e-05):
    m = jnp.mean(x, axis=axis, keepdims=True)
    v = jnp.var(x, axis=axis, keepdims=True)
    return (x - m) / jnp.sqrt(v + eps)

def _scatter_add(tgt, idx, src, axis=0):
    return tgt.at[idx].add(src)

def _segment_sum(src, seg, n):
    return jax.ops.segment_sum(src, seg, n)
kernel_name = 'mk_macaron_d1_jaxref_r8_b4170c'

def setup_inputs(seed: int=0):
    np.random.seed(seed)
    _w = jnp.asarray

    def _L0_attn_setup():
        import jax, jax.numpy as jnp
        import numpy as np
        DIM = 128
        HEADS = 16
        DIM_HEAD = 64
        INNER = HEADS * DIM_HEAD

        def _attention(x, ln_gamma, ln_beta, w_qkv, w_out, b_out):
            b, n, _ = x.shape
            scale = DIM_HEAD ** (-0.5)
            mu = jnp.mean(x, axis=-1, keepdims=True)
            var = jnp.var(x, axis=-1, keepdims=True)
            xn = (x - mu) / jnp.sqrt(var + 1e-05) * ln_gamma + ln_beta
            qkv = jnp.einsum('bnd,ed->bne', xn, w_qkv)
            q, k, v = jnp.split(qkv, 3, axis=-1)
            reshape = lambda t: t.reshape(b, n, HEADS, DIM_HEAD).transpose(0, 2, 1, 3)
            q, k, v = (reshape(q) * scale, reshape(k), reshape(v))
            sim = jnp.einsum('bhid,bhjd->bhij', q, k)
            mask_value = -jnp.finfo(sim.dtype).max
            causal = jnp.triu(jnp.ones((n, n), dtype=bool), k=1)
            sim = jnp.where(causal, mask_value, sim)
            sim = sim - jax.lax.stop_gradient(jnp.max(sim, axis=-1, keepdims=True))
            attn = jax.nn.softmax(sim, axis=-1)
            out = jnp.einsum('bhij,bhjd->bhid', attn, v)
            out = out.transpose(0, 2, 1, 3).reshape(b, n, INNER)
            return jnp.einsum('bne,de->bnd', out, w_out) + b_out
        key = jax.random.key(seed)
        ks = jax.random.split(key, 6)
        x = jax.random.normal(ks[0], (2, 256, DIM), dtype=jnp.float32)
        ln_gamma = jnp.ones((DIM,), dtype=jnp.float32)
        ln_beta = jnp.zeros((DIM,), dtype=jnp.float32)
        w_qkv = jax.random.normal(ks[1], (3 * INNER, DIM), dtype=jnp.float32) * DIM ** (-0.5)
        w_out = jax.random.normal(ks[2], (DIM, INNER), dtype=jnp.float32) * INNER ** (-0.5)
        b_out = jax.random.normal(ks[3], (DIM,), dtype=jnp.float32) * 0.02
        return {'x': x, 'ln_gamma': ln_gamma, 'ln_beta': ln_beta, 'w_qkv': w_qkv, 'w_out': w_out, 'b_out': b_out}
    _L0_attn_in = _L0_attn_setup()

    def _L0_ffn_setup():
        import jax, jax.numpy as jnp
        import numpy as np
        DIM = 128
        HIDDEN = 384
        SCALE = 1.0 / 127.0

        def _dequant(w_int, dtype):
            return w_int.astype(dtype) * jnp.asarray(SCALE, dtype)
        key = jax.random.key(seed)
        k_x, k_g, k_u, k_d = jax.random.split(key, 4)
        x = jax.random.normal(k_x, (4, 256, DIM), dtype=jnp.float32)
        w_gate = jax.random.randint(k_g, (HIDDEN, DIM), -127, 128, dtype=jnp.int32)
        w_up = jax.random.randint(k_u, (HIDDEN, DIM), -127, 128, dtype=jnp.int32)
        w_down = jax.random.randint(k_d, (DIM, HIDDEN), -127, 128, dtype=jnp.int32)
        return {'x': x, 'w_gate': w_gate, 'w_up': w_up, 'w_down': w_down}
    _L0_ffn_in = _L0_ffn_setup()
    _d = {'L0_attn_x': _L0_attn_in['x'], 'L0_attn_ln_gamma': _L0_attn_in['ln_gamma'], 'L0_attn_ln_beta': _L0_attn_in['ln_beta'], 'L0_attn_w_qkv': _L0_attn_in['w_qkv'], 'L0_attn_w_out': _L0_attn_in['w_out'], 'L0_attn_b_out': _L0_attn_in['b_out'], 'L0_ffn_w_gate': _L0_ffn_in['w_gate'], 'L0_ffn_w_up': _L0_ffn_in['w_up'], 'L0_ffn_w_down': _L0_ffn_in['w_down']}
    _x0 = _d['L0_attn_x']
    _d['L0_attn_x'] = jax.random.normal(jax.random.fold_in(jax.random.key(seed), 1), (8, 512, 128), dtype=_x0.dtype)
    del _x0
    return _d

def reference(L0_attn_x, L0_attn_ln_gamma, L0_attn_ln_beta, L0_attn_w_qkv, L0_attn_w_out, L0_attn_b_out, L0_ffn_w_gate, L0_ffn_w_up, L0_ffn_w_down):

    def _L0_attn_ref(x, ln_gamma, ln_beta, w_qkv, w_out, b_out):
        import jax, jax.numpy as jnp
        import numpy as np
        DIM = 128
        HEADS = 16
        DIM_HEAD = 64
        INNER = HEADS * DIM_HEAD

        def _attention(x, ln_gamma, ln_beta, w_qkv, w_out, b_out):
            b, n, _ = x.shape
            scale = DIM_HEAD ** (-0.5)
            mu = jnp.mean(x, axis=-1, keepdims=True)
            var = jnp.var(x, axis=-1, keepdims=True)
            xn = (x - mu) / jnp.sqrt(var + 1e-05) * ln_gamma + ln_beta
            qkv = jnp.einsum('bnd,ed->bne', xn, w_qkv)
            q, k, v = jnp.split(qkv, 3, axis=-1)
            reshape = lambda t: t.reshape(b, n, HEADS, DIM_HEAD).transpose(0, 2, 1, 3)
            q, k, v = (reshape(q) * scale, reshape(k), reshape(v))
            sim = jnp.einsum('bhid,bhjd->bhij', q, k)
            mask_value = -jnp.finfo(sim.dtype).max
            causal = jnp.triu(jnp.ones((n, n), dtype=bool), k=1)
            sim = jnp.where(causal, mask_value, sim)
            sim = sim - jax.lax.stop_gradient(jnp.max(sim, axis=-1, keepdims=True))
            attn = jax.nn.softmax(sim, axis=-1)
            out = jnp.einsum('bhij,bhjd->bhid', attn, v)
            out = out.transpose(0, 2, 1, 3).reshape(b, n, INNER)
            return jnp.einsum('bne,de->bnd', out, w_out) + b_out
        return _attention(x, ln_gamma, ln_beta, w_qkv, w_out, b_out)

    def _L0_ffn_ref(x, w_gate, w_up, w_down):
        import jax, jax.numpy as jnp
        import numpy as np
        DIM = 128
        HIDDEN = 384
        SCALE = 1.0 / 127.0

        def _dequant(w_int, dtype):
            return w_int.astype(dtype) * jnp.asarray(SCALE, dtype)
        wg = _dequant(w_gate, x.dtype)
        wu = _dequant(w_up, x.dtype)
        wd = _dequant(w_down, x.dtype)
        gate = jnp.einsum('bsd,hd->bsh', x, wg)
        up = jnp.einsum('bsd,hd->bsh', x, wu)
        h = jax.nn.silu(gate) * up
        return jnp.einsum('bsh,dh->bsd', h, wd)
    x = L0_attn_x
    x = x + 0.5 * _L0_ffn_ref(_layernorm(x, axis=-1), L0_ffn_w_gate, L0_ffn_w_up, L0_ffn_w_down)
    x = x + _L0_attn_ref(_layernorm(x, axis=-1), L0_attn_ln_gamma, L0_attn_ln_beta, L0_attn_w_qkv, L0_attn_w_out, L0_attn_b_out)
    x = x + 0.5 * _L0_ffn_ref(_layernorm(x, axis=-1), L0_ffn_w_gate, L0_ffn_w_up, L0_ffn_w_down)
    return x

_drawn_inputs = setup_inputs


def setup_inputs(seed=0):
    import zlib

    import numpy as np

    out = dict(_drawn_inputs(seed))
    spreads = {'L0_attn_ln_gamma': (1.0, 0.6), 'L0_attn_ln_beta': (0.0, 0.8)}
    factors = {'L0_attn_w_qkv': 8.0, 'L0_attn_w_out': 8.0, 'L0_attn_b_out': 200.0}
    for name, (base, spread) in spreads.items():
        noise = np.random.default_rng([zlib.crc32(name.encode()), seed]).standard_normal(out[name].shape)
        drawn = base * np.exp(spread * noise) if base else spread * noise
        out[name] = jnp.asarray(drawn.astype(out[name].dtype))
    for name, factor in factors.items():
        out[name] = (out[name] * factor).astype(out[name].dtype)
    return out
```

```python
import concourse.bass as bass
from concourse import mybir
from contextlib import ExitStack


def macaron_block_kernel(nc, x, ln_gamma, ln_beta, w_qkv, w_out, b_out, w_gate, w_up, w_down, out):
    fp32, fp32r, bf16, i32 = mybir.dt.float32, mybir.dt.float32r, mybir.dt.bfloat16, mybir.dt.int32
    ALU, ACT, AX = mybir.AluOpType, mybir.ActivationFunctionType, mybir.AxisListType

    P = 128
    BATCH, SEQ, D = x.shape
    assert D == P
    QT = SEQ // P
    INNER = w_out.shape[1]
    DH = 64
    HEADS = INNER // DH
    PAIRS = HEADS // 2
    HID = w_gate.shape[0]
    HJ = HID // P
    SCALE_INT8 = 1.0 / 127.0
    SM_SCALE = DH ** -0.5
    EPS = 1e-5
    MASKED = -3.0e38
    WJ = 3 * HJ
    NPREP = 13
    POFF = [0, P, 3 * P, 6 * P]
    PCOLS = 10 * P
    TOFF = [P, 5 * P, 8 * P, 10 * P]
    TCOLS = 11 * P
    TGROUPS = [(P, [(0, q) for q in range(4)]),
               (5 * P, [(1, q) for q in range(1, 4)]),
               (8 * P, [(2, 2), (2, 3), (3, 3)])]

    x_v = x.rearrange("b (t p) d -> p (b t) d", p=P)
    out_v = out.rearrange("b (t p) d -> p (b t) d", p=P)

    ctx = ExitStack()
    with ctx:
        def sb(name, shape, dt=fp32):
            return ctx.enter_context(nc.sbuf_tensor(name, shape, dt))

        def sem(name):
            return ctx.enter_context(nc.semaphore(name))

        ident = sb("ident", [P, P])
        ident_bf = sb("ident_bf", [P, P], bf16)
        mask_bf = sb("mask_bf", [P, 2 * P], bf16)
        zero_bf = sb("zero_bf", [P, SEQ], bf16)
        minus_half = sb("minus_half", [P, QT])
        gamma = sb("gamma", [P, 1])
        beta = sb("beta", [P, 1])
        bout = sb("bout", [P, 1])
        wqkv_sb = sb("wqkv_sb", [P, 3 * INNER // P, P])
        wo_sb = sb("wo_sb", [P, INNER])
        wffn_i = sb("wffn_i", [P, WJ * P], i32)
        wffn_f = sb("wffn_f", [P, WJ * P])
        wffn_hi = sb("wffn_hi", [P, WJ * P], fp32r)
        wffn_lo = sb("wffn_lo", [P, WJ * P], fp32r)
        woT = sb("woT", [P, INNER])
        m_hi = sb("m_hi", [P, HEADS * P], fp32r)
        m_lo = sb("m_lo", [P, HEADS * P], fp32r)
        n_hi = sb("n_hi", [P, HEADS * P], fp32r)
        n_lo = sb("n_lo", [P, HEADS * P], fp32r)
        xres = sb("xres", [P, BATCH * QT, D])
        xa_hi = sb("xa_hi", [P, BATCH * SEQ], fp32r)
        xa_lo = sb("xa_lo", [P, BATCH * SEQ], fp32r)
        KINDS = ("ffn", "outer", "inner")
        bnst = {k: sb(f"bnst_{k}", [P, QT, 6]) for k in KINDS}
        bnmv = {k: sb(f"bnmv_{k}", [P, QT, 2]) for k in KINDS}
        vareps = {k: sb(f"vareps_{k}", [P, QT]) for k in KINDS}
        rstd = {k: sb(f"rstd_{k}", [P, QT]) for k in KINDS}
        xn = {k: sb(f"xn_{k}", [P, QT, D]) for k in KINDS}
        xT_hi = sb("xT_hi", [P, SEQ], fp32r)
        xT_lo = sb("xT_lo", [P, SEQ], fp32r)
        silu_g = sb("silu_g", [P, 2, SEQ])
        h_f = sb("h_f", [P, 2, SEQ])
        h_hi = sb("h_hi", [P, HJ, SEQ], fp32r)
        h_lo = sb("h_lo", [P, HJ, SEQ], fp32r)
        yT = sb("yT", [P, SEQ])
        xa_f = sb("xa_f", [P, SEQ])
        m_st = sb("m_st", [P, 2, 2 * P], fp32r)
        xs = sb("xs", [P, 2, SEQ], fp32r)
        t_hi = [sb(f"t_hi{h}", [P, SEQ], fp32r) for h in range(2)]
        t_lo = [sb(f"t_lo{h}", [P, SEQ], fp32r) for h in range(2)]
        u_hi = sb("u_hi", [P, QT, 2, P], fp32r)
        u_lo = sb("u_lo", [P, QT, 2, P], fp32r)
        negm = [sb(f"negm{h}", [P, QT]) for h in range(2)]
        rsum = [sb(f"rsum{h}", [P, QT]) for h in range(2)]
        rrec = [sb(f"rrec{h}", [P, QT]) for h in range(2)]
        prob = [wqkv_sb[:, :, :].rearrange("p r d -> p (r d)")[:, h * PCOLS:(h + 1) * PCOLS] for h in range(2)]
        pt_hi = [sb(f"pt_hi{h}", [P, TCOLS], fp32r) for h in range(2)]
        pt_lo = [sb(f"pt_lo{h}", [P, TCOLS], fp32r) for h in range(2)]

        bank = [ctx.enter_context(nc.psum_tensor(f"bank{i}", [P, SEQ], fp32)) for i in range(8)]
        b_xT, b_g, b_u, b_d, b_back, b_xa = bank[0], bank[1:3], bank[3:5], bank[5], bank[6], bank[7]
        b_s01, b_s2, b_s3 = bank[0], bank[1], bank[2]
        b_t = [bank[3], bank[4]]
        b_x = [bank[5], bank[6]]
        b_y = bank[7]
        SBANK = {3: (b_s3, 0, 4 * P), 2: (b_s2, 0, 3 * P), 1: (b_s01, 2 * P, 2 * P), 0: (b_s01, 0, 2 * P)}

        s_ld_ffn, s_ld_x, s_ld_attn = sem("ld_ffn"), sem("ld_x"), sem("ld_attn")
        s_ident, s_mask, s_zero = sem("ident_ready"), sem("mask_ready"), sem("zeros_ready")
        s_wf = sem("ffn_w_scaled")
        s_pp, s_ph, s_pl = sem("prep_product"), sem("prep_hi"), sem("prep_lo")
        s_st = {k: sem(f"stats_{k}") for k in KINDS}
        s_mv = {k: sem(f"meanvar_{k}") for k in KINDS}
        s_ve = {k: sem(f"vareps_{k}") for k in KINDS}
        s_rs = {k: sem(f"rstd_{k}") for k in KINDS}
        s_xn = {k: sem(f"normed_{k}") for k in KINDS}
        s_xT, s_xh, s_xl = sem("xT_psum"), sem("xT_hi"), sem("xT_lo")
        s_gate, s_up, s_silu, s_h = sem("gate"), sem("up"), sem("silu"), sem("h")
        s_hh, s_hl, s_dn, s_yT = sem("h_hi"), sem("h_lo"), sem("down"), sem("ffn_yT")
        s_bk, s_x1 = sem("ffn_back"), sem("ffn_added")
        s_xaT, s_xaf, s_xah, s_xal = sem("xa_psum"), sem("xa_f"), sem("xa_hi"), sem("xa_lo")
        s_mst, s_xs = sem("m_staged"), sem("xs_staged")
        s_t, s_u, s_xhi, s_xlo = sem("t_done"), sem("u_done"), sem("tu_hi"), sem("tu_lo")
        s_s, s_max, s_exp, s_rc, s_nrm = sem("scores"), sem("maxima"), sem("exps"), sem("recips"), sem("probs")
        s_T, s_phi, s_plo, s_pv = sem("probsT"), sem("pt_hi"), sem("pt_lo"), sem("pv")
        s_y, s_yb, s_fin = sem("attn_yT"), sem("attn_back"), sem("attn_added")
        s_out = sem("stored")
        s_held = sem("held")

        def four_heads(t, i):
            return t[:, :].rearrange("p (g k h c) -> p g k h c", g=2, k=4, h=2)[:, i // 2, :, i % 2, :]

        def four(b):
            return b[:, :].rearrange("p (k c) -> p k c", k=4)

        def seq_slice(t, b):
            return t[:, bass.ds(b * SEQ, SEQ)]

        def tiles(b):
            return xres[:, bass.ds(b * QT, QT), :]

        def attention_loop(eng, pair, finish):
            pair(0, 0, 0, False, None)
            with eng.Fori(0, BATCH - 1) as b:
                with eng.Fori(1, PAIRS) as j:
                    pair(b, j, b * PAIRS + j, True, None)
                pair(b + 1, 0, b * PAIRS + PAIRS, True, b)
            with eng.Fori(1, PAIRS) as j:
                pair(BATCH - 1, j, j + (BATCH - 1) * PAIRS, True, None)
            finish()

        block = ctx.enter_context(nc.Block())

        @block.sync
        def _(sp):
            wi = wffn_i[:, :].rearrange("p (w d) -> p w d", d=P)
            sp.dma_start(wi[:, 0:HJ, :], w_gate.rearrange("(j p) d -> p j d", p=P)).then_inc(s_ld_ffn, 16)
            sp.dma_start(wi[:, HJ:2 * HJ, :], w_up.rearrange("(j p) d -> p j d", p=P)).then_inc(s_ld_ffn, 16)
            sp.dma_start(wffn_i[:, 2 * HID:3 * HID], w_down).then_inc(s_ld_ffn, 16)
            sp.dma_start(xres[:, :, :], x_v).then_inc(s_ld_x, 16)
            sp.dma_start(wo_sb[:, :], w_out).then_inc(s_ld_attn, 16)
            sp.dma_start(wqkv_sb[:, :, :], w_qkv.rearrange("(r p) d -> p r d", p=P)).then_inc(s_ld_attn, 16)

            sp.wait_ge(s_pl, NPREP - 2)
            sp.wait_ge(s_xal, BATCH)
            def stage_m(j, n):
                if not isinstance(n, int):
                    sp.wait_ge(s_t, 2 * n)
                sp.dma_start(m_st[:, 0, :].bitcast(fp32), m_hi[:, bass.ds(j * 2 * P, 2 * P)].bitcast(fp32)).then_inc(s_mst, 16)
                sp.dma_start(m_st[:, 1, :].bitcast(fp32), m_lo[:, bass.ds(j * 2 * P, 2 * P)].bitcast(fp32)).then_inc(s_mst, 16)

            def stage_x(b):
                if not isinstance(b, int):
                    sp.wait_ge(s_u, 2 * PAIRS * b)
                sp.dma_start(xs[:, 0, :].bitcast(fp32), seq_slice(xa_hi, b).bitcast(fp32)).then_inc(s_xs, 16)
                sp.dma_start(xs[:, 1, :].bitcast(fp32), seq_slice(xa_lo, b).bitcast(fp32)).then_inc(s_xs, 16)

            stage_m(0, 0)
            stage_x(0)
            with sp.Fori(1, PAIRS) as j:
                stage_m(j, j)
            with sp.Fori(1, BATCH) as b:
                stage_m(0, b * PAIRS)
                stage_x(b)
                with sp.Fori(1, PAIRS) as j:
                    stage_m(j, b * PAIRS + j)

            with sp.Fori(0, BATCH) as c:
                sp.wait_ge(s_x1, c + (BATCH + 1))
                sp.dma_start(out_v[:, bass.ds(c * QT, QT), :], tiles(c)).then_inc(s_out, 16)
            sp.wait_ge(s_out, 16 * BATCH)

        @block.gpsimd
        def _(pool):
            pool.memset(ident[:, :], 0.0).then_inc(s_ident, 1)
            pool.memset(mask_bf[:, :], 0.0).then_inc(s_mask, 1)
            pool.wait_ge(s_ident, 1)
            pool.affine_select(out=ident[:, :], in_=ident[:, :], compare_op=ALU.not_equal, fill=1.0,
                               base=0, pattern=[[-1, P]], channel_multiplier=1).then_inc(s_ident, 1)
            pool.wait_ge(s_mask, 1)
            pool.affine_select(out=mask_bf[:, :], in_=mask_bf[:, :], compare_op=ALU.is_ge, fill=MASKED,
                               base=0, pattern=[[-1, 2 * P]], channel_multiplier=1).then_inc(s_mask, 1)
            pool.wait_ge(s_ident, 2)
            pool.tensor_copy(ident_bf[:, :], ident[:, :]).then_inc(s_mask, 1)
            pool.memset(zero_bf[:, :], 0.0).then_inc(s_zero, 1)
            for h in range(2):
                pool.memset(pt_hi[h][:, 0:P].bitcast(fp32), 0.0).then_inc(s_zero, 1)
                pool.memset(pt_lo[h][:, 0:P].bitcast(fp32), 0.0).then_inc(s_zero, 1)
            pool.memset(minus_half[:, :], -0.5).then_inc(s_zero, 1)
            pool.wait_ge(s_zero, 6)

            def rsqrt(k, i):
                pool.wait_ge(s_ve[k], i + 1)
                pool.tensor_tensor(rstd[k][:, :], vareps[k][:, :], minus_half[:, :], ALU.pow).then_inc(s_rs[k], 1)

            with pool.Fori(0, BATCH) as c:
                for k in KINDS:
                    rsqrt(k, c)

            def normalise(h, k):
                for i, q in enumerate((3, 2, 1, 0)):
                    cols = prob[h][:, POFF[q]:POFF[q] + P * (q + 1)]
                    pool.wait_ge(s_rc, 4 * k + (i + 1))
                    pool.sem_inc(s_held, 1)
                    pool.tensor_scalar(cols, cols, rrec[h][:, q:q + 1], 1.0, ALU.mult, ALU.mult).then_inc(s_nrm, 1)

            with pool.Fori(0, BATCH * PAIRS) as n:
                for h in range(2):
                    normalise(h, 2 * n + h)

            with pool.Fori(BATCH, 2 * BATCH) as c:
                rsqrt("ffn", c)

        @block.scalar
        def _(act):
            act.dma_start(gamma[:, :], ln_gamma.rearrange("(p a) -> p a", a=1)).then_inc(s_ld_attn, 16)
            act.dma_start(beta[:, :], ln_beta.rearrange("(p a) -> p a", a=1)).then_inc(s_ld_attn, 16)
            act.dma_start(bout[:, :], b_out.rearrange("(p a) -> p a", a=1)).then_inc(s_ld_attn, 16)

            for i in range(3):
                cols = slice(i * SEQ, min((i + 1) * SEQ, WJ * P))
                act.wait_ge(s_pp, i + 1)
                act.activation(wffn_hi[:, cols], bank[i][:, 0:cols.stop - cols.start], ACT.Copy).then_inc(s_ph, 1)
            for i in range(4):
                act.wait_ge(s_pp, i + 4)
                act.activation(four_heads(m_hi, i), four(bank[i + 3]), ACT.Copy, scale=SM_SCALE).then_inc(s_ph, 1)
            for i in range(2):
                act.wait_ge(s_pp, i + 8)
                act.activation(woT[:, i * SEQ:(i + 1) * SEQ], bank[(i + 7) % 8][:, :], ACT.Copy).then_inc(s_ph, 1)
            for i in range(4):
                act.wait_ge(s_pp, i + 10)
                act.activation(four_heads(n_hi, i), four(bank[i + 1]), ACT.Copy).then_inc(s_ph, 1)

            def ffn(c):
                act.wait_ge(s_xT, c + 1)
                act.activation(xT_hi[:, :], b_xT[:, :], ACT.Copy).then_inc(s_xh, 1)
                for j in range(HJ):
                    act.wait_ge(s_gate, HJ * c + (j + 1))
                    act.activation(silu_g[:, j % 2, :], b_g[j % 2][:, :], ACT.Silu).then_inc(s_silu, 1)
                    act.wait_ge(s_h, HJ * c + (j + 1))
                    act.activation(h_hi[:, j, :], h_f[:, j % 2, :], ACT.Copy).then_inc(s_hh, 1)
                act.wait_ge(s_dn, c + 1)
                act.activation(yT[:, :], b_d[:, :], ACT.Copy).then_inc(s_yT, 1)

            with act.Fori(0, BATCH) as c:
                ffn(c)
                act.wait_ge(s_xaf, c + 1)
                act.activation(seq_slice(xa_hi, c), xa_f[:, :], ACT.Copy).then_inc(s_xah, 1)

            def pt_split(h, k):
                if not isinstance(k, int) or k > 1:
                    act.wait_ge(s_pv, k - 1)
                for g, (off, blocks) in enumerate(TGROUPS):
                    w = P * len(blocks)
                    act.wait_ge(s_T, 3 * k + (g + 1))
                    act.activation(pt_hi[h][:, off:off + w], b_t[g % 2][:, 0:w], ACT.Copy).then_inc(s_phi, 1)

            def softmax(h, k):
                if not isinstance(k, int) or k > 1:
                    act.wait_ge(s_T, 3 * k - 3)
                for i, q in enumerate((3, 2, 1, 0)):
                    sbank, off, _ = SBANK[q]
                    act.wait_ge(s_max, 3 * k + min(i + 1, 3))
                    act.activation(prob[h][:, POFF[q]:POFF[q] + P * (q + 1)], sbank[:, off:off + P * (q + 1)],
                                   ACT.Exp, bias=negm[h][:, q:q + 1], scale=1.0,
                                   accum_out=rsum[h][:, q:q + 1]).then_inc(s_exp, 1)

            def attn_y(b):
                act.wait_ge(s_pv, HEADS * (b + 1))
                act.activation(yT[:, :], b_y[:, :], ACT.Identity, bias=bout[:, :], scale=1.0).then_inc(s_y, 1)

            def pair(b, j, n, tail, done):
                for h in range(2):
                    act.wait_ge(s_t, 2 * n + (h + 1))
                    if tail:
                        act.wait_ge(s_s, 6 * n - 3 + 3 * h)
                    act.activation(t_hi[h][:, :], b_x[h][:, :], ACT.Copy).then_inc(s_xhi, 1)
                if tail:
                    pt_split(1, 2 * n - 1)
                softmax(0, 2 * n)
                if done is not None:
                    attn_y(done)
                if tail:
                    act.wait_ge(s_pv, 2 * n)
                for i in range(2):
                    act.wait_ge(s_u, 2 * n + (i + 1))
                    act.activation(u_hi[:, 2 * i:2 * i + 2, :, :].rearrange("p k h d -> p (k h d)"),
                                   b_x[i][:, :], ACT.Copy).then_inc(s_xhi, 1)
                pt_split(0, 2 * n)
                softmax(1, 2 * n + 1)

            def finish():
                pt_split(1, BATCH * HEADS - 1)
                attn_y(BATCH - 1)

            attention_loop(act, pair, finish)

            with act.Fori(BATCH, 2 * BATCH) as c:
                ffn(c)

        @block.vector
        def _(dve):
            dve.wait_ge(s_ld_ffn, 48)
            dve.tensor_scalar(wffn_f[:, :], wffn_i[:, :], SCALE_INT8, None, ALU.mult).then_inc(s_wf, 1)
            dve.wait_ge(s_ld_x, 16)
            for i in range(3):
                cols = slice(i * SEQ, min((i + 1) * SEQ, WJ * P))
                dve.wait_ge(s_ph, i + 1)
                dve.tensor_tensor(wffn_lo[:, cols], bank[i][:, 0:cols.stop - cols.start],
                                  wffn_hi[:, cols].bitcast(fp32), ALU.subtract).then_inc(s_pl, 1)
            for i in range(4):
                dve.wait_ge(s_ph, i + 4)
                dve.scalar_tensor_tensor(four_heads(m_lo, i), four(bank[i + 3]), SM_SCALE,
                                         four_heads(m_hi, i).bitcast(fp32), ALU.mult, ALU.subtract).then_inc(s_pl, 1)
            for i in range(4):
                dve.wait_ge(s_ph, i + 10)
                dve.tensor_tensor(four_heads(n_lo, i), four(bank[i + 1]), four_heads(n_hi, i).bitcast(fp32),
                                  ALU.subtract).then_inc(s_pl, 1)

            def layer_norm(k, i, src):
                dve.sem_inc(s_held, 1)
                for t in range(QT):
                    last = dve.bn_stats(bnst[k][:, t, :], src(t))
                last.then_inc(s_st[k], 1)
                dve.wait_ge(s_st[k], i + 1)
                dve.sem_inc(s_held, 1)
                for t in range(QT):
                    last = dve.bn_aggr(bnmv[k][:, t, :], bnst[k][:, t, :])
                last.then_inc(s_mv[k], 1)
                dve.wait_ge(s_mv[k], i + 1)
                dve.tensor_scalar(vareps[k][:, :], bnmv[k][:, :, 1], EPS, None, ALU.add).then_inc(s_ve[k], 1)
                dve.wait_ge(s_rs[k], i + 1)
                for t in range(QT):
                    last = dve.tensor_scalar(xn[k][:, t, :], src(t), bnmv[k][:, t, 0:1], rstd[k][:, t:t + 1],
                                             ALU.subtract, ALU.mult)
                last.then_inc(s_xn[k], 1)

            def ffn(c, chunk):
                def src(t):
                    return xres[:, bass.ds(chunk * QT + t, 1), :].rearrange("p a d -> p (a d)")

                layer_norm("ffn", c, src)
                dve.wait_ge(s_xh, c + 1)
                dve.tensor_tensor(xT_lo[:, :], b_xT[:, :], xT_hi[:, :].bitcast(fp32), ALU.subtract).then_inc(s_xl, 1)
                for j in range(HJ):
                    dve.wait_ge(s_silu, HJ * c + (j + 1))
                    dve.wait_ge(s_up, HJ * c + (j + 1))
                    dve.tensor_tensor(h_f[:, j % 2, :], silu_g[:, j % 2, :], b_u[j % 2][:, :],
                                      ALU.mult).then_inc(s_h, 1)
                    dve.wait_ge(s_hh, HJ * c + (j + 1))
                    dve.tensor_tensor(h_lo[:, j, :], h_f[:, j % 2, :], h_hi[:, j, :].bitcast(fp32),
                                      ALU.subtract).then_inc(s_hl, 1)
                dve.wait_ge(s_bk, c + 1)
                dve.scalar_tensor_tensor(tiles(chunk).rearrange("p t d -> p (t d)"), b_back[:, :], 0.5,
                                         tiles(chunk).rearrange("p t d -> p (t d)"),
                                         ALU.mult, ALU.add).then_inc(s_x1, 1)
                return src

            dve.wait_ge(s_ld_attn, 80)
            with dve.Fori(0, BATCH) as c:
                src = ffn(c, c)
                dve.wait_ge(s_x1, c + 1)
                layer_norm("outer", c, src)
                dve.wait_ge(s_xn["outer"], c + 1)
                layer_norm("inner", c, lambda t: xn["outer"][:, t, :])
                dve.wait_ge(s_xaT, c + 1)
                dve.tensor_scalar(xa_f[:, :], b_xa[:, :], gamma[:, :], beta[:, :], ALU.mult, ALU.add).then_inc(s_xaf, 1)
                dve.wait_ge(s_xah, c + 1)
                dve.tensor_tensor(seq_slice(xa_lo, c), xa_f[:, :], seq_slice(xa_hi, c).bitcast(fp32),
                                  ALU.subtract).then_inc(s_xal, 1)

            def pt_split(h, k):
                for g, (off, blocks) in enumerate(TGROUPS):
                    w = P * len(blocks)
                    dve.wait_ge(s_phi, 3 * k + (g + 1))
                    dve.tensor_tensor(pt_lo[h][:, off:off + w], b_t[g % 2][:, 0:w],
                                      pt_hi[h][:, off:off + w].bitcast(fp32), ALU.subtract).then_inc(s_plo, 1)

            def softmax(h, k):
                dve.wait_ge(s_s, 3 * k + 1)
                dve.tensor_reduce(negm[h][:, 3:4], b_s3[:, :], axis=AX.X, op=ALU.max, negate=True).then_inc(s_max, 1)
                dve.wait_ge(s_s, 3 * k + 2)
                dve.tensor_reduce(negm[h][:, 2:3], b_s2[:, 0:3 * P], axis=AX.X, op=ALU.max,
                                  negate=True).then_inc(s_max, 1)
                dve.wait_ge(s_s, 3 * k + 3)
                dve.tensor_reduce(negm[h][:, 0:2], b_s01[:, :].rearrange("p (q k) -> p q k", q=2), axis=AX.X,
                                  op=ALU.max, negate=True).then_inc(s_max, 1)
                for i, q in enumerate((3, 2, 1, 0)):
                    dve.wait_ge(s_exp, 4 * k + (i + 1))
                    dve.reciprocal(rrec[h][:, q:q + 1], rsum[h][:, q:q + 1]).then_inc(s_rc, 1)

            def attn_add(b):
                dve.wait_ge(s_yb, b + 1)
                dve.tensor_tensor(tiles(b).rearrange("p t d -> p (t d)"), b_t[1][:, :],
                                  tiles(b).rearrange("p t d -> p (t d)"), ALU.add).then_inc(s_fin, 1)

            def pair(b, j, n, tail, done):
                for h in range(2):
                    dve.wait_ge(s_xhi, 4 * n + (h + 1))
                    dve.tensor_tensor(t_lo[h][:, :], b_x[h][:, :], t_hi[h][:, :].bitcast(fp32),
                                      ALU.subtract).then_inc(s_xlo, 1)
                if tail:
                    pt_split(1, 2 * n - 1)
                softmax(0, 2 * n)
                for i in range(2):
                    rows = slice(2 * i, 2 * i + 2)
                    dve.wait_ge(s_xhi, 4 * n + (i + 3))
                    dve.tensor_tensor(u_lo[:, rows, :, :].rearrange("p k h d -> p (k h d)"), b_x[i][:, :],
                                      u_hi[:, rows, :, :].rearrange("p k h d -> p (k h d)").bitcast(fp32),
                                      ALU.subtract).then_inc(s_xlo, 1)
                if done is not None:
                    attn_add(done)
                pt_split(0, 2 * n)
                softmax(1, 2 * n + 1)

            def finish():
                pt_split(1, BATCH * HEADS - 1)
                attn_add(BATCH - 1)

            attention_loop(dve, pair, finish)
            dve.wait_ge(s_fin, BATCH)

            with dve.Fori(0, BATCH) as c:
                ffn(c + BATCH, c)

        @block.tensor
        def _(pe):
            def split_product(dst, lhs, rhs, start=True, stop=True):
                pe.matmul(dst, lhs[0], rhs[1], start=start, stop=False)
                pe.matmul(dst, lhs[1], rhs[0], start=False, stop=False)
                return pe.matmul(dst, lhs[0], rhs[0], start=False, stop=stop)

            pe.wait_ge(s_ident, 2)
            pe.wait_ge(s_wf, 1)
            for i in range(3):
                for k in range(4 * i, min(4 * i + 4, WJ)):
                    last = pe.transpose(bank[i][:, (k - 4 * i) * P:(k - 4 * i + 1) * P],
                                        wffn_f[:, k * P:(k + 1) * P], ident[:, :])
                last.then_inc(s_pp, 1)
            pe.wait_ge(s_ld_attn, 80)

            def head_rows(part, head):
                return wqkv_sb[DH * (head % 2):DH * (head % 2) + DH, part * PAIRS + head // 2, :]

            for i in range(4):
                for k in range(4):
                    head = 8 * (i // 2) + 2 * k + i % 2
                    last = pe.matmul(bank[i + 3][:, k * P:(k + 1) * P], head_rows(0, head), head_rows(1, head),
                                     start=True, stop=True)
                last.then_inc(s_pp, 1)
            for i in range(2):
                if i:
                    pe.wait_ge(s_pl, i)
                for k in range(4):
                    last = pe.transpose(bank[(i + 7) % 8][:, k * P:(k + 1) * P],
                                        wo_sb[:, (4 * i + k) * P:(4 * i + k + 1) * P], ident[:, :])
                last.then_inc(s_pp, 1)
            pe.wait_ge(s_ph, 9)
            for i in range(4):
                pe.wait_ge(s_pl, i + 2)
                for k in range(4):
                    head = 8 * (i // 2) + 2 * k + i % 2
                    half = slice(DH * (head % 2), DH * (head % 2) + DH)
                    last = pe.matmul(bank[i + 1][:, k * P:(k + 1) * P], head_rows(2, head),
                                     woT[half, (head // 2) * P:(head // 2 + 1) * P], start=True, stop=True)
                last.then_inc(s_pp, 1)
            pe.wait_ge(s_pl, NPREP - 2)

            def transpose4(dst, src):
                for t in range(QT):
                    last = pe.transpose(dst[:, t * P:(t + 1) * P], src(t), ident[:, :])
                return last

            def ffn_w(part, j):
                cols = slice((part * HJ + j) * P, (part * HJ + j + 1) * P)
                return wffn_hi[:, cols], wffn_lo[:, cols]

            def ffn(c, first):
                pe.wait_ge(s_xn["ffn"], c + 1)
                transpose4(b_xT, lambda t: xn["ffn"][:, t, :]).then_inc(s_xT, 1)
                pe.wait_ge(s_xl, c + 1)
                for j in range(HJ):
                    if j >= 2:
                        pe.wait_ge(s_h, HJ * c + (j - 1))
                    split_product(b_g[j % 2][:, :], ffn_w(0, j), (xT_hi[:, :], xT_lo[:, :])).then_inc(s_gate, 1)
                    split_product(b_u[j % 2][:, :], ffn_w(1, j), (xT_hi[:, :], xT_lo[:, :])).then_inc(s_up, 1)
                for j in range(HJ):
                    pe.wait_ge(s_hl, HJ * c + (j + 1))
                    last = split_product(b_d[:, :], ffn_w(2, j), (h_hi[:, j, :], h_lo[:, j, :]),
                                         start=j == 0, stop=j == HJ - 1)
                last.then_inc(s_dn, 1)
                pe.wait_ge(s_yT, c + 1)
                transpose4(b_back, lambda t: yT[:, t * P:(t + 1) * P]).then_inc(s_bk, 1)

            with pe.Fori(0, BATCH) as c:
                ffn(c, True)
                pe.wait_ge(s_xn["inner"], c + 1)
                transpose4(b_xa, lambda t: xn["inner"][:, t, :]).then_inc(s_xaT, 1)
            pe.wait_ge(s_xal, BATCH)
            pe.wait_ge(s_mask, 3)
            pe.wait_ge(s_zero, 6)

            def transpose_probs(h, k, done=None):
                pe.wait_ge(s_nrm, 4 * k + 4)
                for g, (_, blocks) in enumerate(TGROUPS):
                    if g == 0 and (not isinstance(k, int) or k > 0):
                        pe.wait_ge(s_plo, 3 * k)
                    if g == 1 and done is not None:
                        pe.wait_ge(s_fin, done + 1)
                    if g == 2:
                        pe.wait_ge(s_plo, 3 * k + 1)
                    for i, (kt, q) in enumerate(blocks):
                        last = pe.transpose(b_t[g % 2][:, i * P:(i + 1) * P],
                                            prob[h][:, POFF[q] + kt * P:POFF[q] + (kt + 1) * P], ident[:, :])
                    last.then_inc(s_T, 1)

            def scores(h, b, n):
                k = 2 * n + h
                pe.wait_ge(s_xlo, 4 * n + (h + 1))
                for i, q in enumerate((3, 2, 1, 0)):
                    sbank, off, w = SBANK[q]
                    if i < 3 and (not isinstance(k, int) or k > 0):
                        pe.wait_ge(s_exp, 4 * k - 4 + (4 if i == 2 else i + 1))
                    keys = bass.ds(b * SEQ, w)
                    dst = sbank[:, off:off + w]
                    split_product(dst, (t_hi[h][:, q * P:(q + 1) * P], t_lo[h][:, q * P:(q + 1) * P]),
                                  (xa_hi[:, keys], xa_lo[:, keys]), stop=False)
                    last = pe.matmul(sbank[:, off + q * P:off + w], ident_bf[:, :], mask_bf[:, 0:w - q * P],
                                     start=False, stop=True)
                    if i != 2:
                        last.then_inc(s_s, 1)

            def probs_values(h, k, n, first=False, last_of_seq=False, done=None):
                pe.wait_ge(s_plo, 3 * k + 3)
                if h == 0:
                    pe.wait_ge(s_xlo, 4 * n + 4)
                if first:
                    if done is not None:
                        pe.wait_ge(s_y, done + 1)
                    pe.matmul(b_y[:, :], zero_bf[:, 0:P], zero_bf[:, :], start=True, stop=False)
                for kt in range(QT):
                    if kt < QT - 1:
                        q0 = kt * P
                        cols = [pt[h][:, TOFF[kt]:TOFF[kt] + SEQ - q0] for pt in (pt_hi, pt_lo)]
                    else:
                        q0 = (QT - 2) * P
                        cols = [pt[h][:, :].rearrange("p (a c) -> p a c", c=P)[:, 0:TOFF[kt] // P + 1:TOFF[kt] // P, :]
                                for pt in (pt_hi, pt_lo)]
                    dst = b_y[:, q0:SEQ]
                    if kt == QT - 1:
                        dst = dst.rearrange("p (a c) -> p a c", c=P)
                    u = (u_hi[:, kt, h, :], u_lo[:, kt, h, :])
                    last = split_product(dst, u, cols, start=False, stop=False)
                if last_of_seq:
                    last = pe.matmul(b_y[:, :], zero_bf[:, 0:P], zero_bf[:, :], start=False, stop=True)
                last.then_inc(s_pv, 1)

            def values(b, j, n):
                pe.wait_ge(s_xs, 32 * (b + 1))
                for i in range(2):
                    pe.wait_ge(s_xlo, 4 * n + (i + 1))
                    for kt in (2 * i, 2 * i + 1):
                        rows = slice(kt * P, (kt + 1) * P)
                        cols = bass.ds(j * 2 * P, 2 * P)
                        last = split_product(b_x[i][:, (kt % 2) * 2 * P:(kt % 2 + 1) * 2 * P],
                                             (xs[:, 0, rows], xs[:, 1, rows]), (n_hi[:, cols], n_lo[:, cols]))
                    last.then_inc(s_u, 1)

            def attn_back():
                transpose4(b_t[1], lambda t: yT[:, t * P:(t + 1) * P]).then_inc(s_yb, 1)

            def pair(b, j, n, tail, done):
                pe.wait_ge(s_mst, 32 * (n + 1))
                for h in range(2):
                    if tail:
                        pe.wait_ge(s_xlo, 4 * n - 1 + h)
                    cols = slice(h * P, (h + 1) * P)
                    split_product(b_x[h][:, :], (m_st[:, 0, cols], m_st[:, 1, cols]),
                                  (seq_slice(xa_hi, b), seq_slice(xa_lo, b))).then_inc(s_t, 1)
                if tail:
                    transpose_probs(1, 2 * n - 1)
                scores(0, b, n)
                if tail:
                    probs_values(1, 2 * n - 1, n - 1, last_of_seq=done is not None)
                values(b, j, n)
                if done is not None:
                    pe.wait_ge(s_y, done + 1)
                    attn_back()
                transpose_probs(0, 2 * n, done)
                scores(1, b, n)
                probs_values(0, 2 * n, n, first=isinstance(j, int), done=done)

            def finish():
                k = BATCH * HEADS - 1
                transpose_probs(1, k)
                probs_values(1, k, BATCH * PAIRS - 1, last_of_seq=True)
                pe.wait_ge(s_y, BATCH)
                attn_back()

            attention_loop(pe, pair, finish)

            with pe.Fori(BATCH, 2 * BATCH) as c:
                ffn(c, False)


_INS = ['L0_attn_x', 'L0_attn_ln_gamma', 'L0_attn_ln_beta', 'L0_attn_w_qkv', 'L0_attn_w_out', 'L0_attn_b_out',
        'L0_ffn_w_gate', 'L0_ffn_w_up', 'L0_ffn_w_down']


def kernel(**inputs):
    import numpy as _np
    import concourse.bacc as _bacc
    from concourse import mybir as _mybir
    from concourse.bass_utils import run_bass_kernel_spmd as _run

    nc = _bacc.Bacc("TRN2", target_bir_lowering=False, num_devices=1)
    arrays, args = {}, []
    for name in _INS:
        a = _np.ascontiguousarray(inputs[name])
        arrays[f"in_{name}_dram"] = a
        args.append(nc.dram_tensor(f"in_{name}_dram", a.shape, _mybir.dt.from_np(a.dtype), kind="ExternalInput").ap())
    shape = arrays["in_L0_attn_x_dram"].shape
    args.append(nc.dram_tensor("out_0_dram", shape, _mybir.dt.float32, kind="ExternalOutput").ap())
    macaron_block_kernel(nc, *args)
    r = _run(nc, [arrays], core_ids=[0])
    return r.results[0]["out_0_dram"]
```

```python
import concourse.bass as bass
from concourse import mybir
from contextlib import ExitStack


def macaron_block_kernel(nc, x, ln_gamma, ln_beta, w_qkv, w_out, b_out, w_gate, w_up, w_down, out):
    fp32, fp32r, bf16, i32 = mybir.dt.float32, mybir.dt.float32r, mybir.dt.bfloat16, mybir.dt.int32
    ALU, ACT, AX = mybir.AluOpType, mybir.ActivationFunctionType, mybir.AxisListType

    P = 128
    BATCH, SEQ, D = x.shape
    assert D == P
    QT = SEQ // P
    INNER = w_out.shape[1]
    DH = 64
    HEADS = INNER // DH
    PAIRS = HEADS // 2
    HID = w_gate.shape[0]
    HJ = HID // P
    SCALE_INT8 = 1.0 / 127.0
    SM_SCALE = DH ** -0.5
    EPS = 1e-5
    MASKED = -3.0e38
    WJ = 3 * HJ
    NPREP = 13
    POFF = [0, P, 3 * P, 6 * P]
    PCOLS = 10 * P
    TOFF = [P, 5 * P, 8 * P, 10 * P]
    TCOLS = 11 * P
    TGROUPS = [(P, [(0, q) for q in range(4)]),
               (5 * P, [(1, q) for q in range(1, 4)]),
               (8 * P, [(2, 2), (2, 3), (3, 3)])]

    x_v = x.rearrange("b (t p) d -> p (b t) d", p=P)
    out_v = out.rearrange("b (t p) d -> p (b t) d", p=P)

    ctx = ExitStack()
    with ctx:
        def sb(name, shape, dt=fp32):
            return ctx.enter_context(nc.sbuf_tensor(name, shape, dt))

        def sem(name):
            return ctx.enter_context(nc.semaphore(name))

        ident = sb("ident", [P, P])
        ident_bf = sb("ident_bf", [P, P], bf16)
        mask_bf = sb("mask_bf", [P, 2 * P], bf16)
        zero_bf = sb("zero_bf", [P, SEQ], bf16)
        minus_half = sb("minus_half", [P, QT])
        gamma = sb("gamma", [P, 1])
        beta = sb("beta", [P, 1])
        bout = sb("bout", [P, 1])
        wqkv_sb = sb("wqkv_sb", [P, 3 * INNER // P, P])
        wo_sb = sb("wo_sb", [P, INNER])
        wffn_i = sb("wffn_i", [P, WJ * P], i32)
        wffn_f = sb("wffn_f", [P, WJ * P])
        wffn_hi = sb("wffn_hi", [P, WJ * P], fp32r)
        wffn_lo = sb("wffn_lo", [P, WJ * P], fp32r)
        woT = sb("woT", [P, INNER])
        m_hi = sb("m_hi", [P, HEADS * P], fp32r)
        m_lo = sb("m_lo", [P, HEADS * P], fp32r)
        n_hi = sb("n_hi", [P, HEADS * P], fp32r)
        n_lo = sb("n_lo", [P, HEADS * P], fp32r)
        xres = sb("xres", [P, BATCH * QT, D])
        xa_hi = sb("xa_hi", [P, BATCH * SEQ], fp32r)
        xa_lo = sb("xa_lo", [P, BATCH * SEQ], fp32r)
        KINDS = ("ffn", "outer", "inner")
        bnst = {k: sb(f"bnst_{k}", [P, QT, 6]) for k in KINDS}
        bnmv = {k: sb(f"bnmv_{k}", [P, QT, 2]) for k in KINDS}
        vareps = {k: sb(f"vareps_{k}", [P, QT]) for k in KINDS}
        rstd = {k: sb(f"rstd_{k}", [P, QT]) for k in KINDS}
        negmean = sb("negmean", [P, QT])
        nmr = sb("nmr", [P, QT])
        xn = {k: sb(f"xn_{k}", [P, QT, D]) for k in KINDS}
        xT_hi = sb("xT_hi", [P, SEQ], fp32r)
        xT_lo = sb("xT_lo", [P, SEQ], fp32r)
        silu_g = sb("silu_g", [P, 2, SEQ])
        h_f = sb("h_f", [P, 2, SEQ])
        h_hi = sb("h_hi", [P, HJ, SEQ], fp32r)
        h_lo = sb("h_lo", [P, HJ, SEQ], fp32r)
        yT = sb("yT", [P, SEQ])
        xa_f = sb("xa_f", [P, SEQ])
        m_st = sb("m_st", [P, 2, 2 * P], fp32r)
        xs = sb("xs", [P, 2, SEQ], fp32r)
        t_hi = [sb(f"t_hi{h}", [P, SEQ], fp32r) for h in range(2)]
        t_lo = [sb(f"t_lo{h}", [P, SEQ], fp32r) for h in range(2)]
        u_hi = sb("u_hi", [P, QT, 2, P], fp32r)
        u_lo = sb("u_lo", [P, QT, 2, P], fp32r)
        negm = [sb(f"negm{h}", [P, QT]) for h in range(2)]
        rsum = [sb(f"rsum{h}", [P, QT]) for h in range(2)]
        rrec = [sb(f"rrec{h}", [P, QT]) for h in range(2)]
        prob = [wqkv_sb[:, :, :].rearrange("p r d -> p (r d)")[:, h * PCOLS:(h + 1) * PCOLS] for h in range(2)]
        pt_hi = [sb(f"pt_hi{h}", [P, TCOLS], fp32r) for h in range(2)]
        pt_lo = [sb(f"pt_lo{h}", [P, TCOLS], fp32r) for h in range(2)]

        bank = [ctx.enter_context(nc.psum_tensor(f"bank{i}", [P, SEQ], fp32)) for i in range(8)]
        b_xT, b_g, b_u, b_d, b_back, b_xa = bank[0], bank[1:3], bank[3:5], bank[5], bank[6], bank[7]
        b_s01, b_s2, b_s3 = bank[0], bank[1], bank[2]
        b_t = [bank[3], bank[4]]
        b_x = [bank[5], bank[6]]
        b_y = bank[7]
        SBANK = {3: (b_s3, 0, 4 * P), 2: (b_s2, 0, 3 * P), 1: (b_s01, 2 * P, 2 * P), 0: (b_s01, 0, 2 * P)}

        s_ld_ffn, s_ld_x, s_ld_attn = sem("ld_ffn"), sem("ld_x"), sem("ld_attn")
        s_ident, s_mask, s_zero = sem("ident_ready"), sem("mask_ready"), sem("zeros_ready")
        s_wf = sem("ffn_w_scaled")
        s_pp, s_ph, s_pl = sem("prep_product"), sem("prep_hi"), sem("prep_lo")
        s_st = {k: sem(f"stats_{k}") for k in KINDS}
        s_mv = {k: sem(f"meanvar_{k}") for k in KINDS}
        s_ve = {k: sem(f"vareps_{k}") for k in KINDS}
        s_rs = {k: sem(f"rstd_{k}") for k in KINDS}
        s_xn = {k: sem(f"normed_{k}") for k in KINDS}
        s_nmr = sem("minus_mean_rstd")
        s_xT, s_xh, s_xl = sem("xT_psum"), sem("xT_hi"), sem("xT_lo")
        s_gate, s_up, s_silu, s_h = sem("gate"), sem("up"), sem("silu"), sem("h")
        s_hh, s_hl, s_dn, s_yT = sem("h_hi"), sem("h_lo"), sem("down"), sem("ffn_yT")
        s_bk, s_x1 = sem("ffn_back"), sem("ffn_added")
        s_xaT, s_xaf, s_xah, s_xal = sem("xa_psum"), sem("xa_f"), sem("xa_hi"), sem("xa_lo")
        s_mst, s_xs = sem("m_staged"), sem("xs_staged")
        s_t, s_u, s_xhi, s_xlo = sem("t_done"), sem("u_done"), sem("tu_hi"), sem("tu_lo")
        s_s, s_max, s_exp, s_rc, s_nrm = sem("scores"), sem("maxima"), sem("exps"), sem("recips"), sem("probs")
        s_T, s_phi, s_plo, s_pv = sem("probsT"), sem("pt_hi"), sem("pt_lo"), sem("pv")
        s_y, s_yb, s_fin = sem("attn_yT"), sem("attn_back"), sem("attn_added")
        s_out = sem("stored")
        s_held = sem("held")

        def four_heads(t, i):
            return t[:, :].rearrange("p (g k h c) -> p g k h c", g=2, k=4, h=2)[:, i // 2, :, i % 2, :]

        def four(b):
            return b[:, :].rearrange("p (k c) -> p k c", k=4)

        def seq_slice(t, b):
            return t[:, bass.ds(b * SEQ, SEQ)]

        def tiles(b):
            return xres[:, bass.ds(b * QT, QT), :]

        def attention_loop(eng, pair):
            pair(0, 0, tail=False)
            with eng.Fori(0, BATCH - 1) as b:
                with eng.Fori(1, PAIRS) as j:
                    pair(b, b * PAIRS + j)
                pair(b + 1, b * PAIRS + PAIRS, done=b)
            with eng.Fori(1, PAIRS - 1) as j:
                pair(BATCH - 1, j + (BATCH - 1) * PAIRS)
            pair(BATCH - 1, BATCH * PAIRS - 1, nxt=False)

        def ffn_phase(step, eng, m0, tail_steps):
            attn = tail_steps is not None
            last = BATCH - 1
            step(0, m0, prev=False, prev2=False, attn=attn)
            if attn:
                step(1, m0 + 1, prev2=False)
            with eng.Fori(2 if attn else 1, last) as c:
                step(c, c + m0, prev2=attn, attn=attn)
            step(last, m0 + last, nxt=False, prev2=attn, attn=attn)
            step(last + 1, m0 + last + 1, cur=False, nxt=False, prev2=attn, attn=attn)
            if attn:
                tail_steps[0]()
                step(last + 2, m0 + last + 2, cur=False, nxt=False, prev=False)
                tail_steps[1]()

        block = ctx.enter_context(nc.Block())

        @block.sync
        def _(sp):
            wi = wffn_i[:, :].rearrange("p (w d) -> p w d", d=P)
            sp.dma_start(wi[:, 0:HJ, :], w_gate.rearrange("(j p) d -> p j d", p=P)).then_inc(s_ld_ffn, 16)
            sp.dma_start(wi[:, HJ:2 * HJ, :], w_up.rearrange("(j p) d -> p j d", p=P)).then_inc(s_ld_ffn, 16)
            sp.dma_start(wffn_i[:, 2 * HID:3 * HID], w_down).then_inc(s_ld_ffn, 16)
            sp.dma_start(xres[:, :, :], x_v).then_inc(s_ld_x, 16)
            sp.dma_start(wo_sb[:, :], w_out).then_inc(s_ld_attn, 16)
            sp.dma_start(wqkv_sb[:, :, :], w_qkv.rearrange("(r p) d -> p r d", p=P)).then_inc(s_ld_attn, 16)

            sp.wait_ge(s_pl, NPREP - 2)
            sp.wait_ge(s_xal, BATCH)
            def stage_m(j, n):
                if not isinstance(n, int):
                    sp.wait_ge(s_t, 2 * n)
                sp.dma_start(m_st[:, 0, :].bitcast(fp32), m_hi[:, bass.ds(j * 2 * P, 2 * P)].bitcast(fp32)).then_inc(s_mst, 16)
                sp.dma_start(m_st[:, 1, :].bitcast(fp32), m_lo[:, bass.ds(j * 2 * P, 2 * P)].bitcast(fp32)).then_inc(s_mst, 16)

            def stage_x(b):
                if not isinstance(b, int):
                    sp.wait_ge(s_u, 2 * PAIRS * b)
                sp.dma_start(xs[:, 0, :].bitcast(fp32), seq_slice(xa_hi, b).bitcast(fp32)).then_inc(s_xs, 16)
                sp.dma_start(xs[:, 1, :].bitcast(fp32), seq_slice(xa_lo, b).bitcast(fp32)).then_inc(s_xs, 16)

            stage_m(0, 0)
            stage_x(0)
            with sp.Fori(1, PAIRS) as j:
                stage_m(j, j)
            with sp.Fori(1, BATCH) as b:
                stage_m(0, b * PAIRS)
                stage_x(b)
                with sp.Fori(1, PAIRS) as j:
                    stage_m(j, b * PAIRS + j)

            with sp.Fori(0, BATCH) as c:
                sp.wait_ge(s_x1, c + (BATCH + 1))
                sp.dma_start(out_v[:, bass.ds(c * QT, QT), :], tiles(c)).then_inc(s_out, 16)
            sp.wait_ge(s_out, 16 * BATCH)

        @block.gpsimd
        def _(pool):
            pool.memset(ident[:, :], 0.0).then_inc(s_ident, 1)
            pool.memset(mask_bf[:, :], 0.0).then_inc(s_mask, 1)
            pool.wait_ge(s_ident, 1)
            pool.affine_select(out=ident[:, :], in_=ident[:, :], compare_op=ALU.not_equal, fill=1.0,
                               base=0, pattern=[[-1, P]], channel_multiplier=1).then_inc(s_ident, 1)
            pool.wait_ge(s_mask, 1)
            pool.affine_select(out=mask_bf[:, :], in_=mask_bf[:, :], compare_op=ALU.is_ge, fill=MASKED,
                               base=0, pattern=[[-1, 2 * P]], channel_multiplier=1).then_inc(s_mask, 1)
            pool.wait_ge(s_ident, 2)
            pool.tensor_copy(ident_bf[:, :], ident[:, :]).then_inc(s_mask, 1)
            pool.memset(zero_bf[:, :], 0.0).then_inc(s_zero, 1)
            for h in range(2):
                pool.memset(pt_hi[h][:, 0:P].bitcast(fp32), 0.0).then_inc(s_zero, 1)
                pool.memset(pt_lo[h][:, 0:P].bitcast(fp32), 0.0).then_inc(s_zero, 1)
            pool.memset(minus_half[:, :], -0.5).then_inc(s_zero, 1)
            pool.wait_ge(s_zero, 6)

            def rsqrt(k, i):
                pool.wait_ge(s_ve[k], i + 1)
                pool.tensor_tensor(rstd[k][:, :], vareps[k][:, :], minus_half[:, :], ALU.pow).then_inc(s_rs[k], 1)

            rsqrt("ffn", 0)

            def ffn_step(c, m, cur=True, nxt=True, prev=True, prev2=True, attn=True):
                if nxt:
                    rsqrt("ffn", m + 1)
                if prev and attn:
                    rsqrt("outer", c - 1)
                    rsqrt("inner", c - 1)
                    pool.wait_ge(s_rs["inner"], c)
                    pool.tensor_tensor(nmr[:, :], negmean[:, :], rstd["inner"][:, :], ALU.mult).then_inc(s_nmr, 1)

            def nothing():
                pass

            ffn_phase(ffn_step, pool, 0, (nothing, nothing))

            def normalise(h, k):
                for i, q in enumerate((3, 2, 1, 0)):
                    cols = prob[h][:, POFF[q]:POFF[q] + P * (q + 1)]
                    pool.wait_ge(s_rc, 4 * k + (i + 1))
                    pool.sem_inc(s_held, 1)
                    pool.tensor_scalar(cols, cols, rrec[h][:, q:q + 1], 1.0, ALU.mult, ALU.mult).then_inc(s_nrm, 1)

            with pool.Fori(0, BATCH * PAIRS) as n:
                for h in range(2):
                    normalise(h, 2 * n + h)

            rsqrt("ffn", BATCH)
            ffn_phase(ffn_step, pool, BATCH, None)

        @block.scalar
        def _(act):
            act.dma_start(gamma[:, :], ln_gamma.rearrange("(p a) -> p a", a=1)).then_inc(s_ld_attn, 16)
            act.dma_start(beta[:, :], ln_beta.rearrange("(p a) -> p a", a=1)).then_inc(s_ld_attn, 16)
            act.dma_start(bout[:, :], b_out.rearrange("(p a) -> p a", a=1)).then_inc(s_ld_attn, 16)

            for i in range(3):
                cols = slice(i * SEQ, min((i + 1) * SEQ, WJ * P))
                act.wait_ge(s_pp, i + 1)
                act.activation(wffn_hi[:, cols], bank[i][:, 0:cols.stop - cols.start], ACT.Copy).then_inc(s_ph, 1)
            def ffn_step(c, m, cur=True, nxt=True, prev=True, prev2=True, attn=True):
                if cur:
                    for j in range(HJ):
                        act.wait_ge(s_gate, HJ * m + (j + 1))
                        act.activation(silu_g[:, j % 2, :], b_g[j % 2][:, :], ACT.Silu).then_inc(s_silu, 1)
                        if j == HJ - 1 and nxt:
                            act.wait_ge(s_xT, m + 2)
                            act.activation(xT_hi[:, :], b_xT[:, :], ACT.Copy).then_inc(s_xh, 1)
                        act.wait_ge(s_h, HJ * m + (j + 1))
                        act.activation(h_hi[:, j, :], h_f[:, j % 2, :], ACT.Copy).then_inc(s_hh, 1)
                if prev2:
                    act.wait_ge(s_xaf, c - 1)
                    act.activation(seq_slice(xa_hi, c - 2), xa_f[:, :], ACT.Copy).then_inc(s_xah, 1)
                if cur:
                    act.wait_ge(s_dn, m + 1)
                    act.activation(yT[:, :], b_d[:, :], ACT.Copy).then_inc(s_yT, 1)
                if prev and attn:
                    act.wait_ge(s_nmr, c)
                    for t in range(QT):
                        last = act.activation(xn["inner"][:, t, :], xn["outer"][:, t, :], ACT.Identity,
                                              bias=nmr[:, t:t + 1], scale=rstd["inner"][:, t:t + 1])
                    last.then_inc(s_xn["inner"], 1)

            def prepare_m_wo():
                for i in range(4):
                    act.wait_ge(s_pp, i + 4)
                    act.activation(four_heads(m_hi, i), four(bank[i + 3]), ACT.Copy, scale=SM_SCALE).then_inc(s_ph, 1)
                for i in range(2):
                    act.wait_ge(s_pp, i + 8)
                    act.activation(woT[:, i * SEQ:(i + 1) * SEQ], bank[i][:, :], ACT.Copy).then_inc(s_ph, 1)

            def prepare_n():
                for i in range(4):
                    act.wait_ge(s_pp, i + 10)
                    act.activation(four_heads(n_hi, i), four(bank[i + 3]), ACT.Copy).then_inc(s_ph, 1)

            def first_input(m):
                act.wait_ge(s_xT, m + 1)
                act.activation(xT_hi[:, :], b_xT[:, :], ACT.Copy).then_inc(s_xh, 1)

            first_input(0)
            ffn_phase(ffn_step, act, 0, (prepare_m_wo, prepare_n))

            def pt_split(h, k, groups):
                if groups[0] == 0 and (not isinstance(k, int) or k > 1):
                    act.wait_ge(s_pv, k - 1)
                for g in groups:
                    off, w = TGROUPS[g][0], P * len(TGROUPS[g][1])
                    act.wait_ge(s_T, 3 * k + (g + 1))
                    act.activation(pt_hi[h][:, off:off + w], b_t[g % 2][:, 0:w], ACT.Copy).then_inc(s_phi, 1)

            def softmax(h, k):
                if not isinstance(k, int) or k > 1:
                    act.wait_ge(s_T, 3 * k - 3)
                for i, q in enumerate((3, 2, 1, 0)):
                    sbank, off, _ = SBANK[q]
                    act.wait_ge(s_max, 3 * k + min(i + 1, 3))
                    act.activation(prob[h][:, POFF[q]:POFF[q] + P * (q + 1)], sbank[:, off:off + P * (q + 1)],
                                   ACT.Exp, bias=negm[h][:, q:q + 1], scale=1.0,
                                   accum_out=rsum[h][:, q:q + 1]).then_inc(s_exp, 1)

            def attn_y(b):
                act.wait_ge(s_pv, HEADS * (b + 1))
                act.activation(yT[:, :], b_y[:, :], ACT.Identity, bias=bout[:, :], scale=1.0).then_inc(s_y, 1)

            def scores_side(m):
                for h in range(2):
                    act.wait_ge(s_t, 2 * m + (h + 1))
                    if not isinstance(m, int) or m > 0:
                        act.wait_ge(s_s, 6 * m - 3 + 3 * h)
                    act.activation(t_hi[h][:, :], b_x[h][:, :], ACT.Copy).then_inc(s_xhi, 1)

            def pair(b, n, tail=True, done=None, nxt=True):
                if tail:
                    pt_split(1, 2 * n - 1, (2,))
                softmax(0, 2 * n)
                if tail:
                    act.wait_ge(s_pv, 2 * n)
                if done is not None:
                    attn_y(done)
                for i in range(2):
                    act.wait_ge(s_u, 2 * n + (i + 1))
                    act.activation(u_hi[:, 2 * i:2 * i + 2, :, :].rearrange("p k h d -> p (k h d)"),
                                   b_x[i][:, :], ACT.Copy).then_inc(s_xhi, 1)
                pt_split(0, 2 * n, (0, 1))
                pt_split(0, 2 * n, (2,))
                softmax(1, 2 * n + 1)
                if nxt:
                    scores_side(n + 1)
                pt_split(1, 2 * n + 1, (0, 1))

            scores_side(0)
            attention_loop(act, pair)
            pt_split(1, BATCH * HEADS - 1, (2,))
            attn_y(BATCH - 1)

            first_input(BATCH)
            ffn_phase(ffn_step, act, BATCH, None)

        @block.vector
        def _(dve):
            dve.wait_ge(s_ld_ffn, 48)
            dve.tensor_scalar(wffn_f[:, :], wffn_i[:, :], SCALE_INT8, None, ALU.mult).then_inc(s_wf, 1)
            dve.wait_ge(s_ld_x, 16)
            for i in range(3):
                cols = slice(i * SEQ, min((i + 1) * SEQ, WJ * P))
                dve.wait_ge(s_ph, i + 1)
                dve.tensor_tensor(wffn_lo[:, cols], bank[i][:, 0:cols.stop - cols.start],
                                  wffn_hi[:, cols].bitcast(fp32), ALU.subtract).then_inc(s_pl, 1)
            def stats(k, i, src):
                dve.sem_inc(s_held, 1)
                for t in range(QT):
                    last = dve.bn_stats(bnst[k][:, t, :], src(t))
                last.then_inc(s_st[k], 1)
                dve.wait_ge(s_st[k], i + 1)
                dve.sem_inc(s_held, 1)
                for t in range(QT):
                    last = dve.bn_aggr(bnmv[k][:, t, :], bnst[k][:, t, :])
                last.then_inc(s_mv[k], 1)
                dve.wait_ge(s_mv[k], i + 1)
                if k == "inner":
                    dve.tensor_scalar(negmean[:, :], bnmv[k][:, :, 0], -1.0, None, ALU.mult)
                dve.tensor_scalar(vareps[k][:, :], bnmv[k][:, :, 1], EPS, None, ALU.add).then_inc(s_ve[k], 1)

            def norm(k, i, src):
                dve.wait_ge(s_rs[k], i + 1)
                for t in range(QT):
                    last = dve.tensor_scalar(xn[k][:, t, :], src(t), bnmv[k][:, t, 0:1], rstd[k][:, t:t + 1],
                                             ALU.subtract, ALU.mult)
                last.then_inc(s_xn[k], 1)

            def tile_of(chunk):
                return lambda t: xres[:, bass.ds(chunk * QT + t, 1), :].rearrange("p a d -> p (a d)")

            def flat(chunk):
                return tiles(chunk).rearrange("p t d -> p (t d)")

            def input_lo(m):
                dve.wait_ge(s_xh, m + 1)
                dve.tensor_tensor(xT_lo[:, :], b_xT[:, :], xT_hi[:, :].bitcast(fp32), ALU.subtract).then_inc(s_xl, 1)

            def hidden(m, j):
                dve.wait_ge(s_silu, HJ * m + (j + 1))
                dve.wait_ge(s_up, HJ * m + (j + 1))
                dve.tensor_tensor(h_f[:, j % 2, :], silu_g[:, j % 2, :], b_u[j % 2][:, :], ALU.mult).then_inc(s_h, 1)

            def hidden_lo(m, j):
                dve.wait_ge(s_hh, HJ * m + (j + 1))
                dve.tensor_tensor(h_lo[:, j, :], h_f[:, j % 2, :], h_hi[:, j, :].bitcast(fp32),
                                  ALU.subtract).then_inc(s_hl, 1)

            def ffn_step(c, m, cur=True, nxt=True, prev=True, prev2=True, attn=True):
                if nxt:
                    stats("ffn", m + 1, tile_of(c + 1))
                if cur:
                    hidden(m, 0)
                if nxt:
                    norm("ffn", m + 1, tile_of(c + 1))
                if prev:
                    dve.wait_ge(s_bk, m)
                    dve.scalar_tensor_tensor(flat(c - 1), b_back[:, :], 0.5, flat(c - 1),
                                             ALU.mult, ALU.add).then_inc(s_x1, 1)
                if cur:
                    hidden_lo(m, 0)
                if prev and attn:
                    dve.wait_ge(s_x1, c)
                    stats("outer", c - 1, tile_of(c - 1))
                if cur:
                    hidden(m, 1)
                if prev and attn:
                    if not isinstance(c, int) or c > 1:
                        dve.wait_ge(s_xn["inner"], c - 1)
                    norm("outer", c - 1, tile_of(c - 1))
                if cur:
                    hidden_lo(m, 1)
                    hidden(m, 2)
                if nxt:
                    input_lo(m + 1)
                if cur:
                    hidden_lo(m, 2)
                if prev2:
                    if not isinstance(c, int) or c > 2:
                        dve.wait_ge(s_xal, c - 2)
                    dve.wait_ge(s_xaT, c - 1)
                    dve.tensor_scalar(xa_f[:, :], b_xa[:, :], gamma[:, :], beta[:, :],
                                      ALU.mult, ALU.add).then_inc(s_xaf, 1)
                if prev and attn:
                    dve.wait_ge(s_xn["outer"], c)
                    stats("inner", c - 1, lambda t: xn["outer"][:, t, :])
                if prev2:
                    dve.wait_ge(s_xah, c - 1)
                    dve.tensor_tensor(seq_slice(xa_lo, c - 2), xa_f[:, :], seq_slice(xa_hi, c - 2).bitcast(fp32),
                                      ALU.subtract).then_inc(s_xal, 1)

            def prepare_m():
                for i in range(4):
                    dve.wait_ge(s_ph, i + 4)
                    dve.scalar_tensor_tensor(four_heads(m_lo, i), four(bank[i + 3]), SM_SCALE,
                                             four_heads(m_hi, i).bitcast(fp32), ALU.mult, ALU.subtract).then_inc(s_pl, 1)

            def prepare_n():
                for i in range(4):
                    dve.wait_ge(s_ph, i + 10)
                    dve.tensor_tensor(four_heads(n_lo, i), four(bank[i + 3]), four_heads(n_hi, i).bitcast(fp32),
                                      ALU.subtract).then_inc(s_pl, 1)

            dve.wait_ge(s_ld_attn, 80)
            stats("ffn", 0, tile_of(0))
            norm("ffn", 0, tile_of(0))
            input_lo(0)
            ffn_phase(ffn_step, dve, 0, (prepare_m, prepare_n))

            def pt_split(h, k, groups):
                for g in groups:
                    off, w = TGROUPS[g][0], P * len(TGROUPS[g][1])
                    dve.wait_ge(s_phi, 3 * k + (g + 1))
                    dve.tensor_tensor(pt_lo[h][:, off:off + w], b_t[g % 2][:, 0:w],
                                      pt_hi[h][:, off:off + w].bitcast(fp32), ALU.subtract).then_inc(s_plo, 1)

            def maxima(h, k, q):
                rows, i, src = {3: (slice(3, 4), 1, b_s3[:, :]), 2: (slice(2, 3), 2, b_s2[:, 0:3 * P]),
                                1: (slice(0, 2), 3, b_s01[:, :].rearrange("p (q k) -> p q k", q=2))}[q]
                dve.wait_ge(s_s, 3 * k + i)
                dve.tensor_reduce(negm[h][:, rows], src, axis=AX.X, op=ALU.max, negate=True).then_inc(s_max, 1)

            def recip(h, k, q):
                dve.wait_ge(s_exp, 4 * k + (4 - q))
                dve.reciprocal(rrec[h][:, q:q + 1], rsum[h][:, q:q + 1]).then_inc(s_rc, 1)

            def softmax(h, k, tail):
                maxima(h, k, 3)
                maxima(h, k, 2)
                if tail:
                    pt_split(1 - h, k - 1, (2,))
                recip(h, k, 3)
                maxima(h, k, 1)
                for q in (2, 1, 0):
                    recip(h, k, q)

            def attn_add(b):
                dve.wait_ge(s_yb, b + 1)
                dve.tensor_tensor(tiles(b).rearrange("p t d -> p (t d)"), b_t[1][:, :],
                                  tiles(b).rearrange("p t d -> p (t d)"), ALU.add).then_inc(s_fin, 1)

            def scores_side(m):
                for h in range(2):
                    dve.wait_ge(s_xhi, 4 * m + (h + 1))
                    dve.tensor_tensor(t_lo[h][:, :], b_x[h][:, :], t_hi[h][:, :].bitcast(fp32),
                                      ALU.subtract).then_inc(s_xlo, 1)

            def pair(b, n, tail=True, done=None, nxt=True):
                softmax(0, 2 * n, tail)
                for i in range(2):
                    rows = slice(2 * i, 2 * i + 2)
                    dve.wait_ge(s_xhi, 4 * n + (i + 3))
                    dve.tensor_tensor(u_lo[:, rows, :, :].rearrange("p k h d -> p (k h d)"), b_x[i][:, :],
                                      u_hi[:, rows, :, :].rearrange("p k h d -> p (k h d)").bitcast(fp32),
                                      ALU.subtract).then_inc(s_xlo, 1)
                pt_split(0, 2 * n, (0, 1))
                softmax(1, 2 * n + 1, True)
                if done is not None:
                    attn_add(done)
                if nxt:
                    scores_side(n + 1)
                pt_split(1, 2 * n + 1, (0, 1))

            scores_side(0)
            attention_loop(dve, pair)
            pt_split(1, BATCH * HEADS - 1, (2,))
            attn_add(BATCH - 1)
            dve.wait_ge(s_fin, BATCH)

            stats("ffn", BATCH, tile_of(0))
            norm("ffn", BATCH, tile_of(0))
            input_lo(BATCH)
            ffn_phase(ffn_step, dve, BATCH, None)

        @block.tensor
        def _(pe):
            def split_product(dst, lhs, rhs, start=True, stop=True):
                pe.matmul(dst, lhs[0], rhs[1], start=start, stop=False)
                pe.matmul(dst, lhs[1], rhs[0], start=False, stop=False)
                return pe.matmul(dst, lhs[0], rhs[0], start=False, stop=stop)

            pe.wait_ge(s_ident, 2)
            pe.wait_ge(s_wf, 1)
            for i in range(3):
                for k in range(4 * i, min(4 * i + 4, WJ)):
                    last = pe.transpose(bank[i][:, (k - 4 * i) * P:(k - 4 * i + 1) * P],
                                        wffn_f[:, k * P:(k + 1) * P], ident[:, :])
                last.then_inc(s_pp, 1)
            pe.wait_ge(s_pl, 3)

            def transpose4(dst, src):
                for t in range(QT):
                    last = pe.transpose(dst[:, t * P:(t + 1) * P], src(t), ident[:, :])
                return last

            def ffn_input(m):
                pe.wait_ge(s_xn["ffn"], m + 1)
                transpose4(b_xT, lambda t: xn["ffn"][:, t, :]).then_inc(s_xT, 1)

            def ffn_w(part, j):
                cols = slice((part * HJ + j) * P, (part * HJ + j + 1) * P)
                return wffn_hi[:, cols], wffn_lo[:, cols]

            def gate_up(m, j):
                if j >= 2:
                    pe.wait_ge(s_h, HJ * m + (j - 1))
                split_product(b_g[j % 2][:, :], ffn_w(0, j), (xT_hi[:, :], xT_lo[:, :])).then_inc(s_gate, 1)
                split_product(b_u[j % 2][:, :], ffn_w(1, j), (xT_hi[:, :], xT_lo[:, :])).then_inc(s_up, 1)

            def down(m, j):
                pe.wait_ge(s_hl, HJ * m + (j + 1))
                last = split_product(b_d[:, :], ffn_w(2, j), (h_hi[:, j, :], h_lo[:, j, :]),
                                     start=j == 0, stop=j == HJ - 1)
                if j == HJ - 1:
                    last.then_inc(s_dn, 1)

            def ffn_step(c, m, cur=True, nxt=True, prev=True, prev2=True, attn=True):
                if cur:
                    pe.wait_ge(s_xl, m + 1)
                    gate_up(m, 0)
                if prev:
                    pe.wait_ge(s_yT, m)
                    transpose4(b_back, lambda t: yT[:, t * P:(t + 1) * P]).then_inc(s_bk, 1)
                if cur:
                    gate_up(m, 1)
                    gate_up(m, 2)
                if nxt:
                    ffn_input(m + 1)
                if cur:
                    down(m, 0)
                    down(m, 1)
                if prev2:
                    pe.wait_ge(s_xn["inner"], c - 1)
                    if not isinstance(c, int) or c > 2:
                        pe.wait_ge(s_xaf, c - 2)
                    transpose4(b_xa, lambda t: xn["inner"][:, t, :]).then_inc(s_xaT, 1)
                if cur:
                    down(m, 2)

            def head_rows(part, head):
                return wqkv_sb[DH * (head % 2):DH * (head % 2) + DH, part * PAIRS + head // 2, :]

            def heads_of(i):
                return [8 * (i // 2) + 2 * k + i % 2 for k in range(4)]

            def prepare_m_wo():
                pe.wait_ge(s_x1, BATCH)
                pe.wait_ge(s_ld_attn, 80)
                for i in range(4):
                    for k, head in enumerate(heads_of(i)):
                        last = pe.matmul(bank[i + 3][:, k * P:(k + 1) * P], head_rows(0, head), head_rows(1, head),
                                         start=True, stop=True)
                    last.then_inc(s_pp, 1)
                for i in range(2):
                    for k in range(4):
                        last = pe.transpose(bank[i][:, k * P:(k + 1) * P],
                                            wo_sb[:, (4 * i + k) * P:(4 * i + k + 1) * P], ident[:, :])
                    last.then_inc(s_pp, 1)

            def prepare_n():
                pe.wait_ge(s_ph, 9)
                for i in range(4):
                    pe.wait_ge(s_pl, i + 4)
                    for k, head in enumerate(heads_of(i)):
                        half = slice(DH * (head % 2), DH * (head % 2) + DH)
                        last = pe.matmul(bank[i + 3][:, k * P:(k + 1) * P], head_rows(2, head),
                                         woT[half, (head // 2) * P:(head // 2 + 1) * P], start=True, stop=True)
                    last.then_inc(s_pp, 1)

            ffn_input(0)
            ffn_phase(ffn_step, pe, 0, (prepare_m_wo, prepare_n))
            pe.wait_ge(s_xal, BATCH)
            pe.wait_ge(s_pl, NPREP - 2)
            pe.wait_ge(s_mask, 3)
            pe.wait_ge(s_zero, 6)

            def transpose_probs(h, k, groups, done=None):
                for g in groups:
                    if g == 0:
                        pe.wait_ge(s_nrm, 4 * k + 4)
                        if not isinstance(k, int) or k > 0:
                            pe.wait_ge(s_plo, 3 * k)
                    if g == 1 and done is not None:
                        pe.wait_ge(s_fin, done + 1)
                    if g == 2:
                        pe.wait_ge(s_plo, 3 * k + 1)
                    blocks = TGROUPS[g][1]
                    for i, (kt, q) in enumerate(blocks):
                        last = pe.transpose(b_t[g % 2][:, i * P:(i + 1) * P],
                                            prob[h][:, POFF[q] + kt * P:POFF[q] + (kt + 1) * P], ident[:, :])
                    last.then_inc(s_T, 1)

            def scores(h, b, n, tiles_of):
                k = 2 * n + h
                pe.wait_ge(s_xlo, 4 * n + (h + 1))
                for q in tiles_of:
                    sbank, off, w = SBANK[q]
                    if q > 0 and (not isinstance(k, int) or k > 0):
                        pe.wait_ge(s_exp, 4 * k - 4 + {3: 1, 2: 2, 1: 4}[q])
                    keys = bass.ds(b * SEQ, w)
                    split_product(sbank[:, off:off + w], (t_hi[h][:, q * P:(q + 1) * P], t_lo[h][:, q * P:(q + 1) * P]),
                                  (xa_hi[:, keys], xa_lo[:, keys]), stop=False)
                    last = pe.matmul(sbank[:, off + q * P:off + w], ident_bf[:, :], mask_bf[:, 0:w - q * P],
                                     start=False, stop=True)
                    if q != 1:
                        last.then_inc(s_s, 1)

            def probs_values(h, k, n, first=False, last_of_seq=False, done=None):
                pe.wait_ge(s_plo, 3 * k + 3)
                if h == 0:
                    pe.wait_ge(s_xlo, 4 * n + 4)
                if first:
                    if done is not None:
                        pe.wait_ge(s_y, done + 1)
                    pe.matmul(b_y[:, :], zero_bf[:, 0:P], zero_bf[:, :], start=True, stop=False)
                for kt in range(QT):
                    if kt < QT - 1:
                        q0 = kt * P
                        cols = [pt[h][:, TOFF[kt]:TOFF[kt] + SEQ - q0] for pt in (pt_hi, pt_lo)]
                    else:
                        q0 = (QT - 2) * P
                        cols = [pt[h][:, :].rearrange("p (a c) -> p a c", c=P)[:, 0:TOFF[kt] // P + 1:TOFF[kt] // P, :]
                                for pt in (pt_hi, pt_lo)]
                    dst = b_y[:, q0:SEQ]
                    if kt == QT - 1:
                        dst = dst.rearrange("p (a c) -> p a c", c=P)
                    u = (u_hi[:, kt, h, :], u_lo[:, kt, h, :])
                    last = split_product(dst, u, cols, start=False, stop=False)
                if last_of_seq:
                    last = pe.matmul(b_y[:, :], zero_bf[:, 0:P], zero_bf[:, :], start=False, stop=True)
                last.then_inc(s_pv, 1)

            def values(b, n, cols):
                pe.wait_ge(s_xs, 32 * (b + 1))
                for i in range(2):
                    pe.wait_ge(s_xlo, 4 * n + (i + 1))
                    for kt in (2 * i, 2 * i + 1):
                        rows = slice(kt * P, (kt + 1) * P)
                        last = split_product(b_x[i][:, (kt % 2) * 2 * P:(kt % 2 + 1) * 2 * P],
                                             (xs[:, 0, rows], xs[:, 1, rows]), (n_hi[:, cols], n_lo[:, cols]))
                    last.then_inc(s_u, 1)

            def attn_back():
                transpose4(b_t[1], lambda t: yT[:, t * P:(t + 1) * P]).then_inc(s_yb, 1)

            def scores_side(b, m):
                pe.wait_ge(s_mst, 32 * (m + 1))
                for h in range(2):
                    if not isinstance(m, int) or m > 0:
                        pe.wait_ge(s_xlo, 4 * m - 1 + h)
                    cols = slice(h * P, (h + 1) * P)
                    split_product(b_x[h][:, :], (m_st[:, 0, cols], m_st[:, 1, cols]),
                                  (seq_slice(xa_hi, b), seq_slice(xa_lo, b))).then_inc(s_t, 1)

            def pair(b, n, tail=True, done=None, nxt=True):
                scores(0, b, n, (3, 2))
                if tail:
                    transpose_probs(1, 2 * n - 1, (2,))
                scores(0, b, n, (1, 0))
                values(b, n, bass.ds((n % PAIRS) * 2 * P, 2 * P))
                if tail:
                    probs_values(1, 2 * n - 1, n - 1, last_of_seq=done is not None)
                transpose_probs(0, 2 * n, (0, 1))
                scores(1, b, n, (3, 2))
                transpose_probs(0, 2 * n, (2,))
                scores(1, b, n, (1, 0))
                if done is not None:
                    pe.wait_ge(s_plo, 6 * n + 2)
                    pe.wait_ge(s_y, done + 1)
                    attn_back()
                if nxt:
                    scores_side((n + 1) // PAIRS, n + 1)
                probs_values(0, 2 * n, n, first=done is not None or not tail, done=done)
                transpose_probs(1, 2 * n + 1, (0, 1), done)

            scores_side(0, 0)
            attention_loop(pe, pair)
            k = BATCH * HEADS - 1
            transpose_probs(1, k, (2,))
            probs_values(1, k, BATCH * PAIRS - 1, last_of_seq=True)
            pe.wait_ge(s_y, BATCH)
            attn_back()

            ffn_input(BATCH)
            ffn_phase(ffn_step, pe, BATCH, None)


_INS = ['L0_attn_x', 'L0_attn_ln_gamma', 'L0_attn_ln_beta', 'L0_attn_w_qkv', 'L0_attn_w_out', 'L0_attn_b_out',
        'L0_ffn_w_gate', 'L0_ffn_w_up', 'L0_ffn_w_down']


def kernel(**inputs):
    import numpy as _np
    import concourse.bacc as _bacc
    from concourse import mybir as _mybir
    from concourse.bass_utils import run_bass_kernel_spmd as _run

    nc = _bacc.Bacc("TRN2", target_bir_lowering=False, num_devices=1)
    arrays, args = {}, []
    for name in _INS:
        a = _np.ascontiguousarray(inputs[name])
        arrays[f"in_{name}_dram"] = a
        args.append(nc.dram_tensor(f"in_{name}_dram", a.shape, _mybir.dt.from_np(a.dtype), kind="ExternalInput").ap())
    shape = arrays["in_L0_attn_x_dram"].shape
    args.append(nc.dram_tensor("out_0_dram", shape, _mybir.dt.float32, kind="ExternalOutput").ap())
    macaron_block_kernel(nc, *args)
    r = _run(nc, [arrays], core_ids=[0])
    return r.results[0]["out_0_dram"]
```

```python
import concourse.bass as bass
from concourse import mybir
from contextlib import ExitStack


def macaron_block_kernel(nc, x, ln_gamma, ln_beta, w_qkv, w_out, b_out, w_gate, w_up, w_down, out):
    fp32, fp32r, bf16, i32 = mybir.dt.float32, mybir.dt.float32r, mybir.dt.bfloat16, mybir.dt.int32
    ALU, ACT, AX = mybir.AluOpType, mybir.ActivationFunctionType, mybir.AxisListType

    P = 128
    BATCH, SEQ, D = x.shape
    assert D == P
    QT = SEQ // P
    INNER = w_out.shape[1]
    DH = 64
    HEADS = INNER // DH
    PAIRS = HEADS // 2
    HID = w_gate.shape[0]
    HJ = HID // P
    assert HJ == 3
    SCALE_INT8 = 1.0 / 127.0
    SM_SCALE = DH ** -0.5
    EPS = 1e-5
    MASKED = -3.0e38
    WJ = 3 * HJ
    NPREP = 13
    POFF = [0, P, 3 * P, 6 * P]
    PCOLS = 10 * P
    TOFF = [0, 4 * P, 7 * P]
    TCOLS = 9 * P
    TGROUPS = [(0, 4, [(0, q) for q in range(4)]),
               (4 * P, 3, [(1, q) for q in range(1, 4)]),
               (7 * P, 2, [(2, 2), (2, 3), (3, 3)])]

    x_v = x.rearrange("b (t p) d -> p (b t) d", p=P)
    out_v = out.rearrange("b (t p) d -> p (b t) d", p=P)

    ctx = ExitStack()
    with ctx:
        def sb(name, shape, dt=fp32):
            return ctx.enter_context(nc.sbuf_tensor(name, shape, dt))

        def sem(name):
            return ctx.enter_context(nc.semaphore(name))

        ident = sb("ident", [P, P])
        ident_bf = sb("ident_bf", [P, P], bf16)
        mask_bf = sb("mask_bf", [P, 2 * P], bf16)
        zero_bf = sb("zero_bf", [P, SEQ], bf16)
        minus_half = sb("minus_half", [P, QT])
        gamma = sb("gamma", [P, 1])
        beta = sb("beta", [P, 1])
        bout = sb("bout", [P, 1])
        wqkv_sb = sb("wqkv_sb", [P, 3 * INNER // P, P])
        wo_sb = sb("wo_sb", [P, INNER])
        wffn_i = sb("wffn_i", [P, WJ * P], i32)
        wffn_f = sb("wffn_f", [P, WJ * P])
        wffn_hi = sb("wffn_hi", [P, WJ * P], fp32r)
        wffn_lo = sb("wffn_lo", [P, WJ * P], fp32r)
        woT = sb("woT", [P, INNER])
        m_hi = sb("m_hi", [P, HEADS * P], fp32r)
        m_lo = sb("m_lo", [P, HEADS * P], fp32r)
        n_hi = sb("n_hi", [P, HEADS * P], fp32r)
        n_lo = sb("n_lo", [P, HEADS * P], fp32r)
        xres = sb("xres", [P, BATCH * QT, D])
        xa_hi = sb("xa_hi", [P, BATCH * SEQ], fp32r)
        xa_lo = sb("xa_lo", [P, BATCH * SEQ], fp32r)
        KINDS = ("ffn", "attn")
        VAR_EPS = {"ffn": (1.0, EPS), "attn": (1.0 + EPS, EPS * EPS)}
        bnst = {k: sb(f"bnst_{k}", [P, QT, 6]) for k in KINDS}
        bnmv = {k: sb(f"bnmv_{k}", [P, QT, 2]) for k in KINDS}
        vareps = {k: sb(f"vareps_{k}", [P, QT]) for k in KINDS}
        rstd = {k: sb(f"rstd_{k}", [P, QT]) for k in KINDS}
        negmean = {k: sb(f"negmean_{k}", [P, QT]) for k in KINDS}
        nmr = {k: sb(f"nmr_{k}", [P, QT]) for k in KINDS}
        xn = {k: sb(f"xn_{k}", [P, QT, D]) for k in KINDS}
        xT_hi = sb("xT_hi", [P, SEQ], fp32r)
        xT_lo = sb("xT_lo", [P, SEQ], fp32r)
        silu_g = sb("silu_g", [P, 2, SEQ])
        h_f = sb("h_f", [P, 2, SEQ])
        h_hi = sb("h_hi", [P, HJ, SEQ], fp32r)
        h_lo = sb("h_lo", [P, HJ, SEQ], fp32r)
        yT = sb("yT", [P, SEQ])
        table = sb("table", [P, 1])
        xa_f = sb("xa_f", [P, SEQ])
        m_st = sb("m_st", [P, 2, 2 * P], fp32r)
        xv = sb("xv", [P, 2, SEQ], fp32r)
        xq = [xT_hi, xT_lo]
        t_hi = sb("t_hi", [P, QT, 2, P], fp32r)
        t_lo = sb("t_lo", [P, QT, 2, P], fp32r)
        u_hi = [sb("u_hi", [P, QT, 2, P], fp32r),
                h_hi[:, 0:2, :].rearrange("p j (k h d) -> p (j k) h d", k=2, h=2)]
        u_lo = [sb("u_lo", [P, QT, 2, P], fp32r),
                h_lo[:, 0:2, :].rearrange("p j (k h d) -> p (j k) h d", k=2, h=2)]
        u3 = [sb(f"u3_{i}", [P, 2 * P]) for i in range(2)]
        pt3 = [sb(f"pt3_{h}", [P, P]) for h in range(2)]
        negm = sb("negm", [P, 2, QT])
        rsum = sb("rsum", [P, 2, QT])
        rrec = sb("rrec", [P, 2, QT])
        prob = [wqkv_sb[:, :, :].rearrange("p r d -> p (r d)")[:, h * PCOLS:(h + 1) * PCOLS] for h in range(2)]
        pt_hi = [sb(f"pt_hi{h}", [P, TCOLS], fp32r) for h in range(2)]
        pt_lo = [sb(f"pt_lo{h}", [P, TCOLS], fp32r) for h in range(2)]

        bank = [ctx.enter_context(nc.psum_tensor(f"bank{i}", [P, SEQ], fp32)) for i in range(8)]
        b_xT, b_g, b_d, b_back, b_u, b_xa = bank[0], bank[1:3], bank[3], bank[4], bank[5:7], bank[7]
        b_s01, b_s2, b_s3 = bank[0], bank[1], bank[2]
        b_t = [bank[3], bank[4]]
        b_x = [bank[5], bank[6]]
        b_y = bank[7]
        SBANK = {3: (b_s3, lambda h: 0), 2: (b_s2, lambda h: 0), 1: (b_s01, lambda h: 2 * P), 0: (b_s01, lambda h: h * P)}
        S_ORDER = [(0, 3), (0, 2), (0, 0), (1, 3), (1, 2), (1, 1)]
        E_ORDER = [(0, 3), (0, 2), (0, 1), (0, 0), (1, 0), (1, 3), (1, 2), (1, 1)]
        NS, NE = len(S_ORDER), len(E_ORDER)

        def s_count(n, h, q):
            return NS * n + S_ORDER.index((0, 0) if (h, q) in ((0, 1), (1, 0)) else (h, q)) + 1

        def e_count(n, h, q):
            return NE * n + E_ORDER.index((h, q)) + 1

        s_ld_ffn, s_ld_x0, s_ld_x = sem("ld_ffn"), sem("ld_x0"), sem("ld_x")
        s_ld_attn, s_ld_vec = sem("ld_attn"), sem("ld_vectors")
        s_ident, s_mask, s_zero = sem("ident_ready"), sem("mask_ready"), sem("zeros_ready")
        s_wf = sem("ffn_w_scaled")
        s_pp, s_ph, s_pl = sem("prep_product"), sem("prep_hi"), sem("prep_lo")
        s_st = {k: sem(f"stats_{k}") for k in KINDS}
        s_mv = {k: sem(f"meanvar_{k}") for k in KINDS}
        s_ve = {k: sem(f"vareps_{k}") for k in KINDS}
        s_rs = {k: sem(f"rstd_{k}") for k in KINDS}
        s_xn = {k: sem(f"normed_{k}") for k in KINDS}
        s_nmr = {k: sem(f"minus_mean_rstd_{k}") for k in KINDS}
        s_xT, s_xh, s_xl = sem("xT_psum"), sem("xT_hi"), sem("xT_lo")
        s_gate, s_up, s_silu, s_h = sem("gate"), sem("up"), sem("silu"), sem("h")
        s_hh, s_hl, s_hl1 = sem("h_hi"), sem("h_lo_0_2"), sem("h_lo_1")
        s_dn, s_yT = sem("down"), sem("ffn_yT")
        s_bk, s_x1 = sem("ffn_back"), sem("ffn_added")
        s_xaT, s_xaf, s_xah, s_xal = sem("xa_psum"), sem("xa_f"), sem("xa_hi"), sem("xa_lo")
        s_mst, s_xv, s_xq = sem("m_staged"), sem("xv_staged"), sem("xq_staged")
        s_t, s_u, s_xhi, s_xlo = sem("t_done"), sem("u_done"), sem("tu_hi"), sem("tu_lo")
        s_s, s_max, s_exp, s_rc, s_nrm = sem("scores"), sem("maxima"), sem("exps"), sem("recips"), sem("probs")
        s_T, s_phi, s_plo, s_pv = sem("probsT"), sem("pt_hi"), sem("pt_lo"), sem("pv")
        s_y, s_yb, s_fin = sem("attn_yT"), sem("attn_back"), sem("attn_added")
        s_out = sem("stored")
        s_held = sem("held")

        def four_heads(t, i):
            return t[:, :].rearrange("p (g k h c) -> p g k h c", g=2, k=4, h=2)[:, i // 2, :, i % 2, :]

        def four(b):
            return b[:, :].rearrange("p (k c) -> p k c", k=4)

        def seq_slice(t, b):
            return t[:, bass.ds(b * SEQ, SEQ)]

        def tiles(b):
            return xres[:, bass.ds(b * QT, QT), :]

        def attention_loop(eng, pair):
            pair(0, 0, 0, tail=False)
            with eng.Fori(0, BATCH - 1) as b:
                with eng.Fori(0, PAIRS // 2 - 1) as j:
                    pair(1, b, b * PAIRS + 2 * j + 1)
                    pair(0, b, b * PAIRS + 2 * j + 2)
                pair(1, b, b * PAIRS + (PAIRS - 1))
                pair(0, b + 1, b * PAIRS + PAIRS, done=b)
            with eng.Fori(0, PAIRS // 2 - 1) as j:
                pair(1, BATCH - 1, 2 * j + (1 + (BATCH - 1) * PAIRS))
                pair(0, BATCH - 1, 2 * j + (2 + (BATCH - 1) * PAIRS))
            pair(1, BATCH - 1, BATCH * PAIRS - 1, nxt=False)

        def ffn_phase(step, eng, m0, prepare):
            attn = prepare is not None
            last = BATCH - 1
            step(0, m0, prev=False, prev2=False, attn=attn)
            if attn:
                step(1, m0 + 1, prev2=False)
                step(2, m0 + 2)
            with eng.Fori(3 if attn else 1, last - 1) as c:
                step(c, c + m0, prev2=attn, attn=attn)
            step(last - 1, m0 + last - 1, nxt2=False, prev2=attn, attn=attn)
            step(last, m0 + last, nxt=False, nxt2=False, prev2=attn, attn=attn)
            step(last + 1, m0 + last + 1, cur=False, nxt=False, nxt2=False, prev2=attn, attn=attn)
            if attn:
                prepare()

        block = ctx.enter_context(nc.Block())

        @block.sync
        def _(sp):
            sp.dma_start(xres[:, 0:QT, :], x_v[:, 0:QT, :]).then_inc(s_ld_x0, 16)
            wi = wffn_i[:, :].rearrange("p (w d) -> p w d", d=P)
            sp.dma_start(wi[:, 0:HJ, :], w_gate.rearrange("(j p) d -> p j d", p=P)).then_inc(s_ld_ffn, 16)
            sp.dma_start(wffn_i[:, 2 * HID:3 * HID], w_down).then_inc(s_ld_ffn, 16)
            sp.dma_start(xres[:, QT:, :], x_v[:, QT:, :]).then_inc(s_ld_x, 16)
            sp.dma_start(wqkv_sb[:, :, :], w_qkv.rearrange("(r p) d -> p r d", p=P)).then_inc(s_ld_attn, 16)
            sp.dma_start(wo_sb[:, :], w_out).then_inc(s_ld_attn, 16)

            def stage_m(j, n):
                if not isinstance(n, int):
                    sp.wait_ge(s_t, 2 * n)
                else:
                    sp.wait_ge(s_pl, 7)
                sp.dma_start(m_st[:, 0, :].bitcast(fp32), m_hi[:, bass.ds(j * 2 * P, 2 * P)].bitcast(fp32)).then_inc(s_mst, 16)
                sp.dma_start(m_st[:, 1, :].bitcast(fp32), m_lo[:, bass.ds(j * 2 * P, 2 * P)].bitcast(fp32)).then_inc(s_mst, 16)

            def stage_x(b):
                if not isinstance(b, int):
                    sp.wait_ge(s_u, 2 * PAIRS * b)
                else:
                    sp.wait_ge(s_xal, 1)
                sp.dma_start(xv[:, 0, :].bitcast(fp32), seq_slice(xa_hi, b).bitcast(fp32)).then_inc(s_xv, 16)
                sp.dma_start(xv[:, 1, :].bitcast(fp32), seq_slice(xa_lo, b).bitcast(fp32)).then_inc(s_xv, 16)
                if not isinstance(b, int):
                    sp.wait_ge(s_s, NS * PAIRS * b)
                else:
                    sp.wait_ge(s_up, HJ * BATCH)
                sp.dma_start(xq[0][:, :].bitcast(fp32), seq_slice(xa_hi, b).bitcast(fp32)).then_inc(s_xq, 16)
                sp.dma_start(xq[1][:, :].bitcast(fp32), seq_slice(xa_lo, b).bitcast(fp32)).then_inc(s_xq, 16)

            stage_m(0, 0)
            stage_x(0)
            with sp.Fori(1, PAIRS) as j:
                stage_m(j, j)
            sp.wait_ge(s_xal, BATCH)
            with sp.Fori(1, BATCH) as b:
                stage_m(0, b * PAIRS)
                stage_x(b)
                with sp.Fori(1, PAIRS) as j:
                    stage_m(j, b * PAIRS + j)

            with sp.Fori(0, BATCH) as c:
                sp.wait_ge(s_x1, c + (BATCH + 1))
                sp.dma_start(out_v[:, bass.ds(c * QT, QT), :], tiles(c)).then_inc(s_out, 16)
            sp.wait_ge(s_out, 16 * BATCH)

        @block.gpsimd
        def _(pool):
            pool.memset(ident[:, :], 0.0).then_inc(s_ident, 1)
            pool.memset(mask_bf[:, :], 0.0).then_inc(s_mask, 1)
            pool.wait_ge(s_ident, 1)
            pool.affine_select(out=ident[:, :], in_=ident[:, :], compare_op=ALU.not_equal, fill=1.0,
                               base=0, pattern=[[-1, P]], channel_multiplier=1).then_inc(s_ident, 1)
            pool.wait_ge(s_mask, 1)
            mask2 = mask_bf[:, :].rearrange("p (a c) -> p a c", a=2)
            pool.affine_select(out=mask2, in_=mask2, compare_op=ALU.is_ge, fill=MASKED,
                               base=0, pattern=[[0, 2], [-1, P]], channel_multiplier=1).then_inc(s_mask, 1)
            pool.wait_ge(s_ident, 2)
            pool.tensor_copy(ident_bf[:, :], ident[:, :]).then_inc(s_mask, 1)
            pool.memset(zero_bf[:, :], 0.0).then_inc(s_zero, 1)
            pool.memset(minus_half[:, :], -0.5).then_inc(s_zero, 1)
            pool.wait_ge(s_zero, 2)

            def factors(k, i):
                pool.wait_ge(s_ve[k], i + 1)
                pool.tensor_tensor(rstd[k][:, :], vareps[k][:, :], minus_half[:, :], ALU.pow).then_inc(s_rs[k], 1)
                pool.wait_ge(s_rs[k], i + 1)
                pool.tensor_tensor(nmr[k][:, :], negmean[k][:, :], rstd[k][:, :], ALU.mult).then_inc(s_nmr[k], 1)

            def attn_lo(i):
                pool.wait_ge(s_xah, i + 1)
                pool.tensor_tensor(seq_slice(xa_lo, i), xa_f[:, :], seq_slice(xa_hi, i).bitcast(fp32),
                                   ALU.subtract).then_inc(s_xal, 1)

            def ffn_step(c, m, cur=True, nxt=True, nxt2=True, prev=True, prev2=True, attn=True):
                if nxt2:
                    pool.wait_ge(s_xn["ffn"], m + 2)
                    factors("ffn", m + 2)
                if cur and attn:
                    pool.wait_ge(s_hh, HJ * m + 2)
                    pool.tensor_tensor(h_lo[:, 1, :], h_f[:, 1, :], h_hi[:, 1, :].bitcast(fp32),
                                       ALU.subtract).then_inc(s_hl1, 1)
                if prev and attn:
                    if prev2:
                        pool.wait_ge(s_xn["attn"], c - 1)
                    factors("attn", c - 1)
                if prev2:
                    attn_lo(c - 2)

            factors("ffn", 0)
            pool.wait_ge(s_xn["ffn"], 1)
            factors("ffn", 1)
            ffn_phase(ffn_step, pool, 0, lambda: attn_lo(BATCH - 1))

            def normalise(n, h, q):
                cols = prob[h][:, POFF[q]:POFF[q] + P * (q + 1)]
                pool.wait_ge(s_rc, e_count(n, h, q))
                pool.sem_inc(s_held, 1)
                pool.tensor_scalar(cols, cols, rrec[:, h, q:q + 1], 1.0, ALU.mult, ALU.mult).then_inc(s_nrm, 1)

            with pool.Fori(0, BATCH * PAIRS - 1) as n:
                for h, q in E_ORDER:
                    normalise(n, h, q)
            for h, q in E_ORDER[0:5]:
                normalise(BATCH * PAIRS - 1, h, q)
            factors("ffn", BATCH)
            for h, q in E_ORDER[5:]:
                normalise(BATCH * PAIRS - 1, h, q)

            pool.wait_ge(s_xn["ffn"], BATCH + 1)
            factors("ffn", BATCH + 1)
            ffn_phase(ffn_step, pool, BATCH, None)

        @block.scalar
        def _(act):
            wi = wffn_i[:, :].rearrange("p (w d) -> p w d", d=P)
            act.dma_start(wi[:, HJ:2 * HJ, :], w_up.rearrange("(j p) d -> p j d", p=P)).then_inc(s_ld_ffn, 16)
            act.dma_start(gamma[:, :], ln_gamma.rearrange("(p a) -> p a", a=1)).then_inc(s_ld_vec, 16)
            act.dma_start(beta[:, :], ln_beta.rearrange("(p a) -> p a", a=1)).then_inc(s_ld_vec, 16)
            act.dma_start(bout[:, :], b_out.rearrange("(p a) -> p a", a=1)).then_inc(s_ld_vec, 16)

            for i in range(3):
                cols = slice(i * SEQ, min((i + 1) * SEQ, WJ * P))
                act.wait_ge(s_pp, i + 1)
                act.activation(wffn_hi[:, cols], bank[i + 5][:, 0:cols.stop - cols.start], ACT.Copy).then_inc(s_ph, 1)

            def tile_of(chunk):
                return lambda t: xres[:, bass.ds(chunk * QT + t, 1), :].rearrange("p a d -> p (a d)")

            def norm(k, i, src):
                act.wait_ge(s_nmr[k], i + 1)
                for t in range(QT):
                    last = act.activation(xn[k][:, t, :], src(t), ACT.Identity, bias=nmr[k][:, t:t + 1],
                                          scale=rstd[k][:, t:t + 1])
                last.then_inc(s_xn[k], 1)

            def input_hi(m):
                act.wait_ge(s_xT, m + 1)
                act.activation(xT_hi[:, :], b_xT[:, :], ACT.Copy).then_inc(s_xh, 1)

            def attn_norm(i):
                if not isinstance(i, int) or i > 0:
                    act.wait_ge(s_xaT, i)
                norm("attn", i, tile_of(i))

            def attn_hi(i):
                act.wait_ge(s_xaf, i + 1)
                act.activation(seq_slice(xa_hi, i), xa_f[:, :], ACT.Copy).then_inc(s_xah, 1)

            def attn_y(b):
                act.wait_ge(s_pv, HEADS * (b + 1))
                act.activation(yT[:, :], b_y[:, :], ACT.Identity, bias=bout[:, :], scale=1.0).then_inc(s_y, 1)

            def load_table(func):
                act.activation(table[:, :], minus_half[:, 0:1], func)

            def ffn_step(c, m, cur=True, nxt=True, nxt2=True, prev=True, prev2=True, attn=True):
                last_phase_begins = isinstance(m, int) and m == BATCH and not attn

                def hidden(j):
                    act.wait_ge(s_gate, HJ * m + (j + 1))
                    act.activation(silu_g[:, j % 2, :], b_g[j % 2][:, :], ACT.Silu).then_inc(s_silu, 1)

                def hidden_hi(j):
                    act.wait_ge(s_h, HJ * m + (j + 1))
                    act.activation(h_hi[:, j, :], h_f[:, j % 2, :], ACT.Copy).then_inc(s_hh, 1)

                if cur:
                    hidden(0)
                if last_phase_begins:
                    attn_y(BATCH - 1)
                if prev:
                    act.wait_ge(s_dn, m)
                    act.activation(yT[:, :], b_d[:, :], ACT.Copy).then_inc(s_yT, 1)
                if cur:
                    hidden_hi(0)
                    hidden(1)
                if last_phase_begins:
                    norm("ffn", BATCH + 1, tile_of(1))
                if prev2:
                    attn_norm(c - 2)
                if cur:
                    hidden_hi(1)
                    hidden(2)
                if nxt:
                    input_hi(m + 1)
                if cur:
                    hidden_hi(2)
                if nxt2:
                    norm("ffn", m + 2, tile_of(c + 2))
                if prev2:
                    attn_hi(c - 2)

            def prepare_m_wo():
                for i in range(4):
                    act.wait_ge(s_pp, i + 4)
                    act.activation(four_heads(m_hi, i), four(bank[i + 3]), ACT.Copy, scale=SM_SCALE).then_inc(s_ph, 1)
                for i in range(2):
                    act.wait_ge(s_pp, i + 8)
                    act.activation(woT[:, i * SEQ:(i + 1) * SEQ], bank[i][:, :], ACT.Copy).then_inc(s_ph, 1)

            def prepare_n():
                for i in range(4):
                    act.wait_ge(s_pp, i + 10)
                    act.activation(four_heads(n_hi, i), four(bank[i + 3]), ACT.Copy).then_inc(s_ph, 1)

            def prepare():
                prepare_m_wo()
                attn_norm(BATCH - 1)
                load_table(ACT.Exp)
                prepare_n()
                attn_hi(BATCH - 1)

            norm("ffn", 0, tile_of(0))
            act.wait_ge(s_zero, 2)
            load_table(ACT.Silu)
            input_hi(0)
            norm("ffn", 1, tile_of(1))
            ffn_phase(ffn_step, act, 0, prepare)

            def pt_split(h, k, groups):
                if groups[0] == 0 and (not isinstance(k, int) or k > 1):
                    act.wait_ge(s_pv, k - 1)
                for g in groups:
                    off, w = TGROUPS[g][0], P * TGROUPS[g][1]
                    act.wait_ge(s_T, 3 * k + (g + 1))
                    act.activation(pt_hi[h][:, off:off + w], b_t[g % 2][:, 0:w], ACT.Copy).then_inc(s_phi, 1)

            def softmax(h, n):
                for eh, q in (E_ORDER[0:5] if h == 0 else E_ORDER[5:8]):
                    if not isinstance(n, int) or n > 0:
                        if q == 3:
                            act.wait_ge(s_T, 6 * n - 3 + 3 * h)
                        if (eh, q) == (1, 0):
                            act.wait_ge(s_T, 6 * n - 2)
                    sbank, off = SBANK[q]
                    act.wait_ge(s_max, s_count(n, eh, q))
                    act.activation(prob[eh][:, POFF[q]:POFF[q] + P * (q + 1)],
                                   sbank[:, off(eh):off(eh) + P * (q + 1)],
                                   ACT.Exp, bias=negm[:, eh, q:q + 1], scale=1.0,
                                   accum_out=rsum[:, eh, q:q + 1]).then_inc(s_exp, 1)

            def scores_side(m):
                for h in range(2):
                    act.wait_ge(s_t, 2 * m + (h + 1))
                    if not isinstance(m, int) or m > 0:
                        act.wait_ge(s_s, NS * m - (3 if h == 0 else 0))
                    act.activation(t_hi[:, :, h, :], four(b_x[h]), ACT.Copy).then_inc(s_xhi, 1)

            def values_hi(buf, n, i):
                act.wait_ge(s_u, 2 * n + (i + 1))
                rows, w = (slice(0, 2), slice(2, 3))[i], (2 - i) * 2 * P
                act.activation(u_hi[buf][:, rows, :, :].rearrange("p k h d -> p (k h d)"),
                               b_x[i][:, 0:w], ACT.Copy).then_inc(s_xhi, 1)

            def pair(i, b, n, tail=True, done=None, nxt=True):
                if tail:
                    pt_split(1, 2 * n - 1, (2,))
                softmax(0, n)
                values_hi(i, n, 0)
                values_hi(i, n, 1)
                if done is not None:
                    attn_y(done)
                pt_split(0, 2 * n, (0, 1, 2))
                softmax(1, n)
                if nxt:
                    scores_side(n + 1)
                else:
                    norm("ffn", BATCH, tile_of(0))
                    load_table(ACT.Silu)
                pt_split(1, 2 * n + 1, (0, 1))

            scores_side(0)
            attention_loop(act, pair)
            input_hi(BATCH)
            pt_split(1, BATCH * HEADS - 1, (2,))
            ffn_phase(ffn_step, act, BATCH, None)

        @block.vector
        def _(dve):
            def stats_tiles(k, src):
                dve.sem_inc(s_held, 1)
                for t in range(QT):
                    last = dve.bn_stats(bnst[k][:, t, :], src(t))
                last.then_inc(s_st[k], 1)

            def stats_merge(k, i):
                dve.wait_ge(s_st[k], i + 1)
                dve.sem_inc(s_held, 1)
                for t in range(QT):
                    last = dve.bn_aggr(bnmv[k][:, t, :], bnst[k][:, t, :])
                last.then_inc(s_mv[k], 1)

            def stats_end(k, i):
                if not isinstance(i, int) or i > 0:
                    dve.wait_ge(s_nmr[k], i)
                dve.wait_ge(s_mv[k], i + 1)
                dve.tensor_scalar(negmean[k][:, :], bnmv[k][:, :, 0], -1.0, None, ALU.mult)
                dve.tensor_scalar(vareps[k][:, :], bnmv[k][:, :, 1], *VAR_EPS[k], ALU.mult, ALU.add).then_inc(s_ve[k], 1)

            def stats(k, i, src):
                stats_tiles(k, src)
                stats_merge(k, i)
                stats_end(k, i)

            def tile_of(chunk):
                return lambda t: xres[:, bass.ds(chunk * QT + t, 1), :].rearrange("p a d -> p (a d)")

            def flat(chunk):
                return tiles(chunk).rearrange("p t d -> p (t d)")

            def input_lo(m):
                dve.wait_ge(s_xh, m + 1)
                dve.tensor_tensor(xT_lo[:, :], b_xT[:, :], xT_hi[:, :].bitcast(fp32), ALU.subtract).then_inc(s_xl, 1)

            def hidden(m, j):
                dve.wait_ge(s_silu, HJ * m + (j + 1))
                dve.wait_ge(s_up, HJ * m + (j + 1))
                if j == 0 and (not isinstance(m, int) or m > 0):
                    dve.wait_ge(s_hl, 2 * m)
                if j == 2:
                    dve.wait_ge(s_hl, 2 * m + 1)
                dve.tensor_tensor(h_f[:, j % 2, :], silu_g[:, j % 2, :], b_u[j % 2][:, :], ALU.mult).then_inc(s_h, 1)

            def hidden_lo(m, j):
                dve.wait_ge(s_hh, HJ * m + (j + 1))
                dve.tensor_tensor(h_lo[:, j, :], h_f[:, j % 2, :], h_hi[:, j, :].bitcast(fp32),
                                  ALU.subtract).then_inc(s_hl1 if j == 1 else s_hl, 1)

            def attn_add(b):
                dve.wait_ge(s_yb, b + 1)
                dve.tensor_tensor(flat(b), b_t[1][:, :], flat(b), ALU.add).then_inc(s_fin, 1)

            def attn_input(i):
                if not isinstance(i, int) or i > 0:
                    dve.wait_ge(s_xal, i)
                dve.wait_ge(s_xaT, i + 1)
                dve.tensor_scalar(xa_f[:, :], b_xa[:, :], gamma[:, :], beta[:, :],
                                  ALU.mult, ALU.add).then_inc(s_xaf, 1)

            def ffn_step(c, m, cur=True, nxt=True, nxt2=True, prev=True, prev2=True, attn=True):
                last_phase_begins = isinstance(m, int) and m == BATCH and not attn
                if cur:
                    hidden(m, 0)
                if nxt2:
                    stats_tiles("ffn", tile_of(c + 2))
                if cur:
                    hidden_lo(m, 0)
                if nxt2:
                    stats_merge("ffn", m + 2)
                if cur:
                    hidden(m, 1)
                if nxt2:
                    stats_end("ffn", m + 2)
                if last_phase_begins:
                    attn_add(BATCH - 1)
                if prev:
                    dve.wait_ge(s_bk, m)
                    dve.scalar_tensor_tensor(flat(c - 1), b_back[:, :], 0.5, flat(c - 1),
                                             ALU.mult, ALU.add).then_inc(s_x1, 1)
                if prev and attn:
                    dve.wait_ge(s_x1, c)
                    stats_tiles("attn", tile_of(c - 1))
                if cur and not attn:
                    hidden_lo(m, 1)
                if cur:
                    hidden(m, 2)
                if nxt:
                    input_lo(m + 1)
                if prev and attn:
                    stats_merge("attn", c - 1)
                if cur:
                    hidden_lo(m, 2)
                if prev and attn:
                    stats_end("attn", c - 1)
                if prev2:
                    attn_input(c - 2)

            def prepare_m():
                for i in range(4):
                    dve.wait_ge(s_ph, i + 4)
                    dve.scalar_tensor_tensor(four_heads(m_lo, i), four(bank[i + 3]), SM_SCALE,
                                             four_heads(m_hi, i).bitcast(fp32), ALU.mult, ALU.subtract).then_inc(s_pl, 1)

            def prepare_n():
                for i in range(4):
                    dve.wait_ge(s_ph, i + 10)
                    dve.tensor_tensor(four_heads(n_lo, i), four(bank[i + 3]), four_heads(n_hi, i).bitcast(fp32),
                                      ALU.subtract).then_inc(s_pl, 1)

            dve.wait_ge(s_ld_x0, 16)
            stats("ffn", 0, tile_of(0))
            dve.wait_ge(s_ld_ffn, 48)
            dve.tensor_scalar(wffn_f[:, :], wffn_i[:, :], SCALE_INT8, None, ALU.mult).then_inc(s_wf, 1)
            for i in range(3):
                cols = slice(i * SEQ, min((i + 1) * SEQ, WJ * P))
                dve.wait_ge(s_ph, i + 1)
                dve.tensor_tensor(wffn_lo[:, cols], bank[i + 5][:, 0:cols.stop - cols.start],
                                  wffn_hi[:, cols].bitcast(fp32), ALU.subtract).then_inc(s_pl, 1)
            input_lo(0)
            dve.wait_ge(s_ld_x, 16)
            dve.wait_ge(s_ld_vec, 48)
            stats("ffn", 1, tile_of(1))

            def prepare():
                prepare_m()
                prepare_n()
                attn_input(BATCH - 1)

            ffn_phase(ffn_step, dve, 0, prepare)

            def pt_split(h, k, groups):
                for g in groups:
                    off, w = TGROUPS[g][0], P * TGROUPS[g][1]
                    dve.wait_ge(s_phi, 3 * k + (g + 1))
                    if g == 2:
                        dve.tensor_copy(pt3[h][:, :], b_t[0][:, w:w + P])
                    dve.tensor_tensor(pt_lo[h][:, off:off + w], b_t[g % 2][:, 0:w],
                                      pt_hi[h][:, off:off + w].bitcast(fp32), ALU.subtract).then_inc(s_plo, 1)

            def maxima(h, n, q):
                dst = negm[:, :, 0] if q == 0 else negm[:, h, q:q + 1]
                src = {3: b_s3[:, :], 2: b_s2[:, 0:3 * P], 1: b_s01[:, 2 * P:],
                       0: b_s01[:, 0:2 * P].rearrange("p (h k) -> p h k", h=2)}[q]
                dve.wait_ge(s_s, s_count(n, h, q))
                last = dve.tensor_reduce(dst, src, axis=AX.X, op=ALU.max, negate=True)
                if (h, q) != (0, 1):
                    last.then_inc(s_max, 1)

            def recip(n, h, q):
                dve.wait_ge(s_exp, e_count(n, h, q))
                dve.reciprocal(rrec[:, h, q:q + 1], rsum[:, h, q:q + 1]).then_inc(s_rc, 1)

            def values_lo(buf, n, i):
                rows, w = (slice(0, 2), slice(2, 3))[i], (2 - i) * 2 * P
                dve.wait_ge(s_xhi, 4 * n + (i + 3))
                if i == 1:
                    dve.tensor_copy(u3[buf][:, :], b_x[1][:, 2 * P:])
                dve.tensor_tensor(u_lo[buf][:, rows, :, :].rearrange("p k h d -> p (k h d)"), b_x[i][:, 0:w],
                                  u_hi[buf][:, rows, :, :].rearrange("p k h d -> p (k h d)").bitcast(fp32),
                                  ALU.subtract).then_inc(s_xlo, 1)

            def softmax(h, n, tail):
                maxima(h, n, 3)
                maxima(h, n, 2)
                if tail:
                    pt_split(1 - h, 2 * n + h - 1, (1,))
                maxima(h, n, 1)
                recip(n, h, 3)
                if h == 0:
                    maxima(0, n, 0)
                    recip(n, h, 2)
                if tail:
                    pt_split(1 - h, 2 * n + h - 1, (2,))
                if h == 1:
                    recip(n, h, 2)
                recip(n, h, 1)
                if h == 0:
                    recip(n, 0, 0)
                    recip(n, 1, 0)

            def scores_side(m):
                for h in range(2):
                    dve.wait_ge(s_xhi, 4 * m + (h + 1))
                    dve.tensor_tensor(t_lo[:, :, h, :], four(b_x[h]), t_hi[:, :, h, :].bitcast(fp32),
                                      ALU.subtract).then_inc(s_xlo, 1)

            def pair(i, b, n, tail=True, done=None, nxt=True):
                softmax(0, n, tail)
                if not nxt:
                    dve.wait_ge(s_fin, BATCH - 1)
                    stats("ffn", BATCH, tile_of(0))
                values_lo(i, n, 0)
                values_lo(i, n, 1)
                pt_split(0, 2 * n, (0,))
                softmax(1, n, True)
                if done is not None:
                    attn_add(done)
                if nxt:
                    scores_side(n + 1)
                pt_split(1, 2 * n + 1, (0,))

            scores_side(0)
            attention_loop(dve, pair)
            pt_split(1, BATCH * HEADS - 1, (1,))
            input_lo(BATCH)
            pt_split(1, BATCH * HEADS - 1, (2,))
            stats("ffn", BATCH + 1, tile_of(1))
            ffn_phase(ffn_step, dve, BATCH, None)

        @block.tensor
        def _(pe):
            def split_product(dst, lhs, rhs, start=True, stop=True):
                pe.matmul(dst, lhs[0], rhs[1], start=start, stop=False)
                pe.matmul(dst, lhs[1], rhs[0], start=False, stop=False)
                return pe.matmul(dst, lhs[0], rhs[0], start=False, stop=stop)

            pe.wait_ge(s_ident, 2)
            pe.wait_ge(s_wf, 1)
            for i in range(3):
                for k in range(4 * i, min(4 * i + 4, WJ)):
                    last = pe.transpose(bank[i + 5][:, (k - 4 * i) * P:(k - 4 * i + 1) * P],
                                        wffn_f[:, k * P:(k + 1) * P], ident[:, :])
                last.then_inc(s_pp, 1)

            def transpose4(dst, src):
                for t in range(QT):
                    last = pe.transpose(dst[:, t * P:(t + 1) * P], src(t), ident[:, :])
                return last

            def ffn_input(m):
                pe.wait_ge(s_xn["ffn"], m + 1)
                transpose4(b_xT, lambda t: xn["ffn"][:, t, :]).then_inc(s_xT, 1)

            def ffn_w(part, j):
                cols = slice((part * HJ + j) * P, (part * HJ + j + 1) * P)
                return wffn_hi[:, cols], wffn_lo[:, cols]

            def gate_up(m, j):
                if j == 0:
                    pe.wait_ge(s_xl, m + 1)
                if j == 0 and (not isinstance(m, int) or m > 0):
                    pe.wait_ge(s_h, HJ * m)
                if j == 2:
                    pe.wait_ge(s_h, HJ * m + 1)
                split_product(b_g[j % 2][:, :], ffn_w(0, j), (xT_hi[:, :], xT_lo[:, :])).then_inc(s_gate, 1)
                split_product(b_u[j % 2][:, :], ffn_w(1, j), (xT_hi[:, :], xT_lo[:, :])).then_inc(s_up, 1)

            def down(m, j):
                if j == 1:
                    pe.wait_ge(s_hl1, m + 1)
                else:
                    pe.wait_ge(s_hl, 2 * m + (1 if j == 0 else 2))
                last = split_product(b_d[:, :], ffn_w(2, j), (h_hi[:, j, :], h_lo[:, j, :]),
                                     start=j == 0, stop=j == HJ - 1)
                if j == HJ - 1:
                    last.then_inc(s_dn, 1)

            def attn_back(b):
                pe.wait_ge(s_y, b + 1)
                transpose4(b_t[1], lambda t: yT[:, t * P:(t + 1) * P]).then_inc(s_yb, 1)

            def attn_input(i):
                pe.wait_ge(s_xn["attn"], i + 1)
                if not isinstance(i, int) or i > 0:
                    pe.wait_ge(s_xaf, i)
                transpose4(b_xa, lambda t: xn["attn"][:, t, :]).then_inc(s_xaT, 1)

            def ffn_step(c, m, cur=True, nxt=True, nxt2=True, prev=True, prev2=True, attn=True):
                last_phase_begins = isinstance(m, int) and m == BATCH and not attn
                if cur and not last_phase_begins:
                    gate_up(m, 0)
                if prev:
                    down(m - 1, 2)
                if cur:
                    gate_up(m, 1)
                if last_phase_begins:
                    attn_back(BATCH - 1)
                if prev:
                    pe.wait_ge(s_yT, m)
                    if isinstance(m, int) and m == BATCH + 1:
                        pe.wait_ge(s_fin, BATCH)
                    transpose4(b_back, lambda t: yT[:, t * P:(t + 1) * P]).then_inc(s_bk, 1)
                if cur:
                    gate_up(m, 2)
                if nxt:
                    ffn_input(m + 1)
                if cur:
                    down(m, 0)
                if prev2:
                    attn_input(c - 2)
                if cur:
                    down(m, 1)

            def head_rows(part, head):
                return wqkv_sb[DH * (head % 2):DH * (head % 2) + DH, part * PAIRS + head // 2, :]

            def heads_of(i):
                return [8 * (i // 2) + 2 * k + i % 2 for k in range(4)]

            def prepare_m_wo():
                pe.wait_ge(s_x1, BATCH)
                pe.wait_ge(s_ld_attn, 32)
                for i in range(4):
                    for k, head in enumerate(heads_of(i)):
                        last = pe.matmul(bank[i + 3][:, k * P:(k + 1) * P], head_rows(1, head), head_rows(0, head),
                                         start=True, stop=True)
                    last.then_inc(s_pp, 1)
                for i in range(2):
                    for k in range(4):
                        last = pe.transpose(bank[i][:, k * P:(k + 1) * P],
                                            wo_sb[:, (4 * i + k) * P:(4 * i + k + 1) * P], ident[:, :])
                    last.then_inc(s_pp, 1)

            def prepare_n():
                pe.wait_ge(s_ph, 9)
                for i in range(4):
                    pe.wait_ge(s_pl, i + 4)
                    for k, head in enumerate(heads_of(i)):
                        half = slice(DH * (head % 2), DH * (head % 2) + DH)
                        last = pe.matmul(bank[i + 3][:, k * P:(k + 1) * P], head_rows(2, head),
                                         woT[half, (head // 2) * P:(head // 2 + 1) * P], start=True, stop=True)
                    last.then_inc(s_pp, 1)

            ffn_input(0)
            pe.wait_ge(s_pl, 3)

            def prepare():
                prepare_m_wo()
                prepare_n()
                attn_input(BATCH - 1)

            ffn_phase(ffn_step, pe, 0, prepare)
            pe.wait_ge(s_pl, NPREP - 2)
            pe.wait_ge(s_mask, 3)
            pe.wait_ge(s_zero, 2)

            def transpose_probs(h, k, groups, done=None):
                for g in groups:
                    if g == 0:
                        pe.wait_ge(s_nrm, 4 * k + 3)
                        if not isinstance(k, int) or k > 0:
                            pe.wait_ge(s_plo, 3 * k)
                    if g == 1 and done is not None:
                        pe.wait_ge(s_fin, done + 1)
                    if g == 2:
                        pe.wait_ge(s_plo, 3 * k + 1)
                    blocks = TGROUPS[g][2]
                    for i, (kt, q) in (enumerate(blocks) if g > 0 else [(i, blocks[i]) for i in (3, 2, 1 - h, h)]):
                        if g == 0 and i == h:
                            pe.wait_ge(s_nrm, 4 * k + 4)
                        last = pe.transpose(b_t[g % 2][:, i * P:(i + 1) * P],
                                            prob[h][:, POFF[q] + kt * P:POFF[q] + (kt + 1) * P], ident[:, :])
                    last.then_inc(s_T, 1)

            def scores(h, b, n, tiles_of):
                for q in tiles_of:
                    pe.wait_ge(s_xlo, 4 * n + (h + 1 if q > 0 else 2))
                    if h == 0 and q == 3:
                        pe.wait_ge(s_xq, 32 * (b + 1))
                    if h == 1:
                        pe.wait_ge(s_exp, e_count(n, 0, q) if q > 1 else e_count(n, 1, 0))
                    elif not isinstance(n, int) or n > 0:
                        pe.wait_ge(s_exp, NE * n - (q - 1 if q > 0 else 0))
                    sbank, off = SBANK[q]
                    heads, keys = (2, 1) if q == 0 else (1, q + 1)
                    dst = sbank[:, off(h):off(h) + heads * keys * P]
                    t = [v[:, 0, :, :] if q == 0 else v[:, 0:keys, h, :] for v in (t_hi, t_lo)]
                    x = [v[:, q * P:(q + 1) * P] for v in xq]
                    split_product(dst.rearrange("p (a c) -> p a c", c=P), x, t, stop=False)
                    last = pe.matmul(dst[:, q * P:] if q > 0 else dst, ident_bf[:, :], mask_bf[:, 0:heads * P],
                                     start=False, stop=True)
                    if (h, q) != (0, 1):
                        last.then_inc(s_s, 1)

            def probs_values(h, k, buf, n, first=False, last_of_seq=False, done=None):
                pe.wait_ge(s_plo, 3 * k + 2)
                if h == 0:
                    pe.wait_ge(s_xlo, 4 * n + 4)
                if first:
                    if done is not None:
                        pe.wait_ge(s_y, done + 1)
                    pe.matmul(b_y[:, :], zero_bf[:, 0:P], zero_bf[:, :], start=True, stop=False)
                for kt in range(QT - 1):
                    if kt == 2:
                        pe.wait_ge(s_plo, 3 * k + 3)
                    split_product(b_y[:, kt * P:], (u_hi[buf][:, kt, h, :], u_lo[buf][:, kt, h, :]),
                                  [pt[h][:, TOFF[kt]:TOFF[kt] + SEQ - kt * P] for pt in (pt_hi, pt_lo)],
                                  start=False, stop=False)
                last = pe.matmul(b_y[:, (QT - 1) * P:], u3[buf][:, h * P:(h + 1) * P], pt3[h][:, :],
                                 start=False, stop=False)
                if last_of_seq:
                    last = pe.matmul(b_y[:, :], zero_bf[:, 0:P], zero_bf[:, :], start=False, stop=True)
                last.then_inc(s_pv, 1)

            def values(b, n, cols):
                pe.wait_ge(s_xv, 32 * (b + 1))
                for i in range(2):
                    pe.wait_ge(s_xlo, 4 * n + (i + 1))
                    for kt in (2 * i, 2 * i + 1):
                        rows = slice(kt * P, (kt + 1) * P)
                        last = split_product(b_x[i][:, (kt % 2) * 2 * P:(kt % 2 + 1) * 2 * P],
                                             (xv[:, 0, rows], xv[:, 1, rows]), (n_hi[:, cols], n_lo[:, cols]))
                    last.then_inc(s_u, 1)

            def scores_side(b, m):
                pe.wait_ge(s_xal, b + 1)
                pe.wait_ge(s_mst, 32 * (m + 1))
                for h in range(2):
                    if not isinstance(m, int) or m > 0:
                        pe.wait_ge(s_xlo, 4 * m - 1 + h)
                    cols = slice(h * P, (h + 1) * P)
                    split_product(b_x[h][:, :], (m_st[:, 0, cols], m_st[:, 1, cols]),
                                  (seq_slice(xa_hi, b), seq_slice(xa_lo, b))).then_inc(s_t, 1)

            def pair(i, b, n, tail=True, done=None, nxt=True):
                scores(0, b, n, (3, 2))
                if tail:
                    transpose_probs(1, 2 * n - 1, (2,))
                scores(0, b, n, (1, 0))
                values(b, n, bass.ds((n % PAIRS) * 2 * P, 2 * P))
                if tail:
                    probs_values(1, 2 * n - 1, 1 - i, n - 1, last_of_seq=done is not None)
                transpose_probs(0, 2 * n, (0, 1))
                scores(1, b, n, (3, 2))
                transpose_probs(0, 2 * n, (2,))
                scores(1, b, n, (1,))
                if done is not None:
                    pe.wait_ge(s_plo, 6 * n + 2)
                    attn_back(done)
                if nxt:
                    scores_side((n + 1) // PAIRS, n + 1)
                probs_values(0, 2 * n, i, n, first=done is not None or not tail, done=done)
                transpose_probs(1, 2 * n + 1, (0, 1), done)

            scores_side(0, 0)
            attention_loop(pe, pair)
            ffn_input(BATCH)
            k = BATCH * HEADS - 1
            transpose_probs(1, k, (2,))
            gate_up(BATCH, 0)
            probs_values(1, k, 1, BATCH * PAIRS - 1, last_of_seq=True)
            ffn_phase(ffn_step, pe, BATCH, None)


_INS = ['L0_attn_x', 'L0_attn_ln_gamma', 'L0_attn_ln_beta', 'L0_attn_w_qkv', 'L0_attn_w_out', 'L0_attn_b_out',
        'L0_ffn_w_gate', 'L0_ffn_w_up', 'L0_ffn_w_down']


def kernel(**inputs):
    import numpy as _np
    import concourse.bacc as _bacc
    from concourse import mybir as _mybir
    from concourse.bass_utils import run_bass_kernel_spmd as _run

    nc = _bacc.Bacc("TRN2", target_bir_lowering=False, num_devices=1)
    arrays, args = {}, []
    for name in _INS:
        a = _np.ascontiguousarray(inputs[name])
        arrays[f"in_{name}_dram"] = a
        args.append(nc.dram_tensor(f"in_{name}_dram", a.shape, _mybir.dt.from_np(a.dtype), kind="ExternalInput").ap())
    shape = arrays["in_L0_attn_x_dram"].shape
    args.append(nc.dram_tensor("out_0_dram", shape, _mybir.dt.float32, kind="ExternalOutput").ap())
    macaron_block_kernel(nc, *args)
    r = _run(nc, [arrays], core_ids=[0])
    return r.results[0]["out_0_dram"]
```
